# Optimizing a Trainium2 kernel written in Bass

```python
import numpy as np
import jax
import jax.numpy as jnp

def _softmax(x, axis=-1):
    return jax.nn.softmax(x, axis=axis)

def _gelu(x):
    return jax.nn.gelu(x, approximate=True)

def _silu(x):
    return jax.nn.silu(x)

def _sigmoid(x):
    return jax.nn.sigmoid(x)

def _layernorm(x, axis=-1, eps=1e-05):
    m = jnp.mean(x, axis=axis, keepdims=True)
    v = jnp.var(x, axis=axis, keepdims=True)
    return (x - m) / jnp.sqrt(v + eps)

def _scatter_add(tgt, idx, src, axis=0):
    return tgt.at[idx].add(src)

def _segment_sum(src, seg, n):
    return jax.ops.segment_sum(src, seg, n)
kernel_name = 'mk_conv_preact_d4_conv_nchw384_r2_411509'

def setup_inputs(seed: int=0):
    np.random.seed(seed)
    _w = jnp.asarray

    def _rec_inputs():
        import jax
        import jax.numpy as jnp
        _gk = jax.random.key(seed)
        x = -0.0001538 + 1 * jax.random.normal(jax.random.fold_in(_gk, 1), (16, 192, 32, 32), jnp.float32)
        return x
    x = _rec_inputs()

    def _L0_conv_setup():
        import jax, jax.numpy as jnp
        import numpy as np
        DIM = 192
        DIM_HEAD = 32
        NUM_HEAD = DIM // DIM_HEAD
        SCALE = DIM_HEAD ** (-0.5)
        key = jax.random.key(seed)
        k1, k2, k3, k4 = jax.random.split(key, 4)
        x = jax.random.normal(k1, (16, DIM, 32, 32), dtype=jnp.float32)
        qkv_w = jax.random.normal(k2, (3 * DIM, DIM), dtype=jnp.float32) * DIM ** (-0.5)
        proj_w = jax.random.normal(k3, (DIM, DIM), dtype=jnp.float32) * DIM ** (-0.5)
        proj_b = jax.random.normal(k4, (DIM,), dtype=jnp.float32) * 0.01
        return {'x': x, 'qkv_w': qkv_w, 'proj_w': proj_w, 'proj_b': proj_b}
    _L0_conv_all = _L0_conv_setup()
    _L0_conv_in = {k: v for k, v in _L0_conv_all.items() if k in ('qkv_w', 'proj_w', 'proj_b')}
    del _L0_conv_all

    def _L1_conv_setup():
        import jax, jax.numpy as jnp
        import numpy as np
        D_MODEL = 96
        D_STATE = 16
        SSM_RATIO = 2.0
        D_INNER = int(SSM_RATIO * D_MODEL)
        DT_RANK = int(np.ceil(D_MODEL / 16))
        K_GROUP = 4
        BATCH, HH, WW = (4, 32, 32)
        DT_MIN, DT_MAX = (0.001, 0.1)
        LN_EPS = 1e-05

        def _cross_scan(x):
            B, D, H, W = x.shape
            x0 = x.reshape(B, D, H * W)
            x1 = jnp.transpose(x, (0, 1, 3, 2)).reshape(B, D, H * W)
            return jnp.stack([x0, x1, x0[..., ::-1], x1[..., ::-1]], axis=1)

        def _cross_merge(ys, H, W):
            B, K, D, L = ys.shape
            y0 = ys[:, 0]
            y2 = ys[:, 2][..., ::-1]
            yt = ys[:, 1] + ys[:, 3][..., ::-1]
            yt = jnp.transpose(yt.reshape(B, D, W, H), (0, 1, 3, 2)).reshape(B, D, L)
            return y0 + y2 + yt

        def _selective_scan(u, dt, A, Bs, Cs):
            dt_l = jnp.moveaxis(dt, -1, 0)
            u_l = jnp.moveaxis(u, -1, 0)
            B_l = jnp.moveaxis(Bs, -1, 0)
            C_l = jnpp_move = jnp.moveaxis(Cs, -1, 0)

            def step(h, inp):
                dtt, ut, bt, ct = inp
                dA = jnp.exp(dtt[..., None] * A)
                h = h * dA + (dtt * ut)[..., None] * bt[:, :, None, :]
                y = jnp.einsum('bkdn,bkn->bkd', h, ct)
                return (h, y)
            h0 = jnp.zeros(u.shape[:3] + (A.shape[-1],), dtype=u.dtype)
            _, ys = jax.lax.scan(step, h0, (dt_l, u_l, B_l, C_l))
            return jnp.moveaxis(ys, 0, -1)
        key = jax.random.key(seed)
        ks = jax.random.split(key, 6)
        x = jax.random.normal(ks[0], (BATCH, D_INNER, HH, WW), dtype=jnp.float32)
        x_proj_weight = jax.random.normal(ks[1], (K_GROUP, DT_RANK + 2 * D_STATE, D_INNER), dtype=jnp.float32) * D_INNER ** (-0.5)
        dt_projs_weight = jax.random.normal(ks[2], (K_GROUP, D_INNER, DT_RANK), dtype=jnp.float32) * DT_RANK ** (-0.5)
        dt = jnp.exp(jax.random.uniform(ks[3], (K_GROUP, D_INNER)) * (np.log(DT_MAX) - np.log(DT_MIN)) + np.log(DT_MIN))
        dt = jnp.clip(dt, 0.0001, None)
        dt_projs_bias = dt + jnp.log(-jnp.expm1(-dt))
        A = jnp.tile(jnp.arange(1, D_STATE + 1, dtype=jnp.float32)[None, :], (K_GROUP * D_INNER, 1))
        A_logs = jnp.log(A)
        Ds = jnp.ones((K_GROUP * D_INNER,), dtype=jnp.float32)
        ln_weight = jnp.ones((D_INNER,), dtype=jnp.float32)
        ln_bias = jnp.zeros((D_INNER,), dtype=jnp.float32)
        return {'x': x, 'x_proj_weight': x_proj_weight, 'dt_projs_weight': dt_projs_weight, 'dt_projs_bias': dt_projs_bias, 'A_logs': A_logs, 'Ds': Ds, 'ln_weight': ln_weight, 'ln_bias': ln_bias}
    _L1_conv_all = _L1_conv_setup()
    _L1_conv_in = {k: v for k, v in _L1_conv_all.items() if k in ('x_proj_weight', 'dt_projs_weight', 'dt_projs_bias', 'A_logs', 'Ds', 'ln_weight', 'ln_bias')}
    del _L1_conv_all

    def _L2_conv_setup():
        import jax, jax.numpy as jnp
        import numpy as np
        K = 30
        key = jax.random.key(seed)
        k1, k2, k3 = jax.random.split(key, 3)
        b, c, h, w = (32, 192, 56, 56)
        x = jax.random.normal(k1, (b, c, h, w), dtype=jnp.float32)
        fan_in = 1 * 3 * 3
        bound = 1.0 / np.sqrt(fan_in)
        weight = jax.random.uniform(k2, (c, 1, 3, 3), dtype=jnp.float32, minval=-bound, maxval=bound)
        bias = jax.random.uniform(k3, (c,), dtype=jnp.float32, minval=-bound, maxval=bound)
        return {'x': x, 'weight': weight, 'bias': bias}
    _L2_conv_all = _L2_conv_setup()
    _L2_conv_in = {k: v for k, v in _L2_conv_all.items() if k in ('weight', 'bias')}
    del _L2_conv_all

    def _L3_conv_setup():
        import jax, jax.numpy as jnp
        import numpy as np
        D_MODEL = 192
        D_STATE = 32
        D_CONV = 3
        EXPAND = 2
        HEADDIM = 32
        NGROUPS = 1
        CHUNK = 128
        D_INNER = EXPAND * D_MODEL
        NHEADS = D_INNER // HEADDIM
        CONV_DIM = D_INNER + 2 * NGROUPS * D_STATE
        D_IN_PROJ = 2 * D_INNER + 2 * NGROUPS * D_STATE + NHEADS
        EPS = 1e-05

        def _chunk_scan(x, dt, A, Bm, Cm):
            b, l, h, p = x.shape
            nc = l // CHUNK
            xc = x.reshape(b, nc, CHUNK, h, p)
            dtc = dt.reshape(b, nc, CHUNK, h)
            hpg = h // NGROUPS
            Bh = jnp.repeat(Bm.reshape(b, nc, CHUNK, NGROUPS, D_STATE), hpg, axis=3)
            Ch = jnp.repeat(Cm.reshape(b, nc, CHUNK, NGROUPS, D_STATE), hpg, axis=3)
            dA = dtc * A
            dA_cs = jnp.cumsum(dA, axis=2)
            Lmat = jnp.exp(dA_cs[:, :, :, None, :] - dA_cs[:, :, None, :, :])
            causal = jnp.tril(jnp.ones((CHUNK, CHUNK), bool))
            att = jnp.einsum('bcihn,bcjhn->bcijh', Ch, Bh) * Lmat * dtc[:, :, None, :, :]
            att = jnp.where(causal[None, None, :, :, None], att, 0.0)
            y_intra = jnp.einsum('bcijh,bcjhp->bcihp', att, xc)
            decay_to_end = jnp.exp(dA_cs[:, :, -1:, :] - dA_cs)
            states = jnp.einsum('bcjhn,bcjh,bcjhp->bchpn', Bh, decay_to_end * dtc, xc)
            chunk_decay = jnp.exp(dA_cs[:, :, -1, :])

            def step(carry, inp):
                st, dec = inp
                new = carry * dec[:, :, None, None] + st
                return (new, carry)
            init = jnp.zeros((b, h, p, D_STATE), x.dtype)
            _, prevs = jax.lax.scan(step, init, (jnp.moveaxis(states, 1, 0), jnp.moveaxis(chunk_decay, 1, 0)))
            prev_states = jnp.moveaxis(prevs, 0, 1)
            y_inter = jnp.einsum('bcihn,bcih,bchpn->bcihp', Ch, jnp.exp(dA_cs), prev_states)
            return (y_intra + y_inter).reshape(b, l, h, p)
        key = jax.random.key(seed)
        ks = jax.random.split(key, 8)
        B, H, W = (16, 32, 32)
        u = jax.random.normal(ks[0], (B, D_MODEL, H, W), jnp.float32)
        in_proj_w = jax.random.normal(ks[1], (D_IN_PROJ, D_MODEL), jnp.float32) / np.sqrt(D_MODEL)
        conv_w = jax.random.normal(ks[2], (CONV_DIM, 1, D_CONV, D_CONV), jnp.float32) / np.sqrt(D_CONV * D_CONV)
        conv_b = jax.random.normal(ks[3], (CONV_DIM,), jnp.float32) * 0.01
        dt = jnp.exp(jax.random.uniform(ks[4], (NHEADS,)) * (np.log(0.1) - np.log(0.001)) + np.log(0.001))
        dt = jnp.clip(dt, 0.0001, None)
        dt_bias = dt + jnp.log(-jnp.expm1(-dt))
        A_log = jnp.log(jax.random.uniform(ks[5], (NHEADS,), minval=1.0, maxval=16.0))
        D = jnp.ones((NHEADS,), jnp.float32)
        norm_w = jnp.ones((D_INNER,), jnp.float32)
        norm_b = jnp.zeros((D_INNER,), jnp.float32)
        out_proj_w = jax.random.normal(ks[6], (D_MODEL, D_INNER), jnp.float32) / np.sqrt(D_INNER)
        return {'u': u, 'in_proj_w': in_proj_w, 'conv_w': conv_w, 'conv_b': conv_b, 'dt_bias': dt_bias, 'A_log': A_log, 'D': D, 'norm_w': norm_w, 'norm_b': norm_b, 'out_proj_w': out_proj_w}
    _L3_conv_all = _L3_conv_setup()
    _L3_conv_in = {k: v for k, v in _L3_conv_all.items() if k in ('in_proj_w', 'conv_w', 'conv_b', 'dt_bias', 'A_log', 'D', 'norm_w', 'norm_b', 'out_proj_w')}
    del _L3_conv_all
    return {'x': x, 'L0_conv_qkv_w': _L0_conv_in['qkv_w'], 'L0_conv_proj_w': _L0_conv_in['proj_w'], 'L0_conv_proj_b': _L0_conv_in['proj_b'], 'L1_conv_x_proj_weight': _L1_conv_in['x_proj_weight'], 'L1_conv_dt_projs_weight': _L1_conv_in['dt_projs_weight'], 'L1_conv_dt_projs_bias': _L1_conv_in['dt_projs_bias'], 'L1_conv_A_logs': _L1_conv_in['A_logs'], 'L1_conv_Ds': _L1_conv_in['Ds'], 'L1_conv_ln_weight': _L1_conv_in['ln_weight'], 'L1_conv_ln_bias': _L1_conv_in['ln_bias'], 'L2_conv_weight': _L2_conv_in['weight'], 'L2_conv_bias': _L2_conv_in['bias'], 'L3_conv_in_proj_w': _L3_conv_in['in_proj_w'], 'L3_conv_conv_w': _L3_conv_in['conv_w'], 'L3_conv_conv_b': _L3_conv_in['conv_b'], 'L3_conv_dt_bias': _L3_conv_in['dt_bias'], 'L3_conv_A_log': _L3_conv_in['A_log'], 'L3_conv_D': _L3_conv_in['D'], 'L3_conv_norm_w': _L3_conv_in['norm_w'], 'L3_conv_norm_b': _L3_conv_in['norm_b'], 'L3_conv_out_proj_w': _L3_conv_in['out_proj_w']}

def reference(x, L0_conv_qkv_w, L0_conv_proj_w, L0_conv_proj_b, L1_conv_x_proj_weight, L1_conv_dt_projs_weight, L1_conv_dt_projs_bias, L1_conv_A_logs, L1_conv_Ds, L1_conv_ln_weight, L1_conv_ln_bias, L2_conv_weight, L2_conv_bias, L3_conv_in_proj_w, L3_conv_conv_w, L3_conv_conv_b, L3_conv_dt_bias, L3_conv_A_log, L3_conv_D, L3_conv_norm_w, L3_conv_norm_b, L3_conv_out_proj_w):
    import jax
    import jax.numpy as jnp

    def _L0_conv_ref(x, qkv_w, proj_w, proj_b):
        import jax, jax.numpy as jnp
        import numpy as np
        DIM = 192
        DIM_HEAD = 32
        NUM_HEAD = DIM // DIM_HEAD
        SCALE = DIM_HEAD ** (-0.5)
        B, C, H, W = x.shape
        N = H * W
        xt = x.reshape(B, C, N).transpose(0, 2, 1)
        qkv = jnp.einsum('bnc,oc->bno', xt, qkv_w)
        qkv = qkv.reshape(B, N, 3, NUM_HEAD, DIM_HEAD).transpose(2, 0, 3, 1, 4)
        q, k, v = (qkv[0], qkv[1], qkv[2])
        attn = jnp.einsum('bhnd,bhmd->bhnm', q, k) * SCALE
        attn = jax.nn.softmax(attn, axis=-1)
        out = jnp.einsum('bhnm,bhmd->bhnd', attn, v)
        out = out.transpose(0, 2, 1, 3).reshape(B, N, C)
        out = jnp.einsum('bnc,oc->bno', out, proj_w) + proj_b
        return out.transpose(0, 2, 1).reshape(B, C, H, W)

    def _L1_conv_ref(x, x_proj_weight, dt_projs_weight, dt_projs_bias, A_logs, Ds, ln_weight, ln_bias):
        import jax, jax.numpy as jnp
        import numpy as np
        D_MODEL = 96
        D_STATE = 16
        SSM_RATIO = 2.0
        D_INNER = int(SSM_RATIO * D_MODEL)
        DT_RANK = int(np.ceil(D_MODEL / 16))
        K_GROUP = 4
        BATCH, HH, WW = (4, 32, 32)
        DT_MIN, DT_MAX = (0.001, 0.1)
        LN_EPS = 1e-05

        def _cross_scan(x):
            B, D, H, W = x.shape
            x0 = x.reshape(B, D, H * W)
            x1 = jnp.transpose(x, (0, 1, 3, 2)).reshape(B, D, H * W)
            return jnp.stack([x0, x1, x0[..., ::-1], x1[..., ::-1]], axis=1)

        def _cross_merge(ys, H, W):
            B, K, D, L = ys.shape
            y0 = ys[:, 0]
            y2 = ys[:, 2][..., ::-1]
            yt = ys[:, 1] + ys[:, 3][..., ::-1]
            yt = jnp.transpose(yt.reshape(B, D, W, H), (0, 1, 3, 2)).reshape(B, D, L)
            return y0 + y2 + yt

        def _selective_scan(u, dt, A, Bs, Cs):
            dt_l = jnp.moveaxis(dt, -1, 0)
            u_l = jnp.moveaxis(u, -1, 0)
            B_l = jnp.moveaxis(Bs, -1, 0)
            C_l = jnpp_move = jnp.moveaxis(Cs, -1, 0)

            def step(h, inp):
                dtt, ut, bt, ct = inp
                dA = jnp.exp(dtt[..., None] * A)
                h = h * dA + (dtt * ut)[..., None] * bt[:, :, None, :]
                y = jnp.einsum('bkdn,bkn->bkd', h, ct)
                return (h, y)
            h0 = jnp.zeros(u.shape[:3] + (A.shape[-1],), dtype=u.dtype)
            _, ys = jax.lax.scan(step, h0, (dt_l, u_l, B_l, C_l))
            return jnp.moveaxis(ys, 0, -1)
        B, D, H, W = x.shape
        K = x_proj_weight.shape[0]
        N = D_STATE
        R = dt_projs_weight.shape[-1]
        L = H * W
        xs = _cross_scan(x)
        x_dbl = jnp.einsum('bkdl,kcd->bkcl', xs, x_proj_weight)
        dts, Bs, Cs = (x_dbl[:, :, :R], x_dbl[:, :, R:R + N], x_dbl[:, :, R + N:])
        dts = jnp.einsum('bkrl,kdr->bkdl', dts, dt_projs_weight)
        A = -jnp.exp(A_logs.astype(jnp.float32)).reshape(K, D, N)
        dt = jax.nn.softplus(dts.astype(jnp.float32) + dt_projs_bias.astype(jnp.float32)[None, :, :, None])
        u = xs.astype(jnp.float32)
        Bs = Bs.astype(jnp.float32)
        Cs = Cs.astype(jnp.float32)
        ys = _selective_scan(u, dt, A, Bs, Cs)
        ys = ys + Ds.astype(jnp.float32).reshape(K, D)[None, :, :, None] * u
        y = _cross_merge(ys, H, W).reshape(B, D, H, W)
        yc = jnp.transpose(y, (0, 2, 3, 1))
        mu = jnp.mean(yc, axis=-1, keepdims=True)
        var = jnp.mean((yc - mu) ** 2, axis=-1, keepdims=True)
        yc = (yc - mu) * jax.lax.rsqrt(var + LN_EPS) * ln_weight + ln_bias
        y = jnp.transpose(yc, (0, 3, 1, 2)).astype(x.dtype)
        return jax.nn.gelu(y, approximate=False)

    def _L2_conv_ref(x, weight, bias):
        import jax, jax.numpy as jnp
        import numpy as np
        K = 30
        b, c, h, w = x.shape
        scores = jax.lax.conv_general_dilated(x, weight, window_strides=(1, 1), padding='SAME', feature_group_count=c, dimension_numbers=('NCHW', 'OIHW', 'NCHW')) + bias[None, :, None, None]
        scores_flat = scores.reshape(b, c, h * w)
        _, topk_idx = jax.lax.top_k(scores_flat, K)
        bi = jnp.arange(b)[:, None, None]
        ci = jnp.arange(c)[None, :, None]
        mask = jnp.zeros((b, c, h * w), dtype=x.dtype).at[bi, ci, topk_idx].set(1.0)
        return x * mask.reshape(b, c, h, w)

    def _L3_conv_ref(u, in_proj_w, conv_w, conv_b, dt_bias, A_log, D, norm_w, norm_b, out_proj_w):
        import jax, jax.numpy as jnp
        import numpy as np
        D_MODEL = 192
        D_STATE = 32
        D_CONV = 3
        EXPAND = 2
        HEADDIM = 32
        NGROUPS = 1
        CHUNK = 128
        D_INNER = EXPAND * D_MODEL
        NHEADS = D_INNER // HEADDIM
        CONV_DIM = D_INNER + 2 * NGROUPS * D_STATE
        D_IN_PROJ = 2 * D_INNER + 2 * NGROUPS * D_STATE + NHEADS
        EPS = 1e-05

        def _chunk_scan(x, dt, A, Bm, Cm):
            b, l, h, p = x.shape
            nc = l // CHUNK
            xc = x.reshape(b, nc, CHUNK, h, p)
            dtc = dt.reshape(b, nc, CHUNK, h)
            hpg = h // NGROUPS
            Bh = jnp.repeat(Bm.reshape(b, nc, CHUNK, NGROUPS, D_STATE), hpg, axis=3)
            Ch = jnp.repeat(Cm.reshape(b, nc, CHUNK, NGROUPS, D_STATE), hpg, axis=3)
            dA = dtc * A
            dA_cs = jnp.cumsum(dA, axis=2)
            Lmat = jnp.exp(dA_cs[:, :, :, None, :] - dA_cs[:, :, None, :, :])
            causal = jnp.tril(jnp.ones((CHUNK, CHUNK), bool))
            att = jnp.einsum('bcihn,bcjhn->bcijh', Ch, Bh) * Lmat * dtc[:, :, None, :, :]
            att = jnp.where(causal[None, None, :, :, None], att, 0.0)
            y_intra = jnp.einsum('bcijh,bcjhp->bcihp', att, xc)
            decay_to_end = jnp.exp(dA_cs[:, :, -1:, :] - dA_cs)
            states = jnp.einsum('bcjhn,bcjh,bcjhp->bchpn', Bh, decay_to_end * dtc, xc)
            chunk_decay = jnp.exp(dA_cs[:, :, -1, :])

            def step(carry, inp):
                st, dec = inp
                new = carry * dec[:, :, None, None] + st
                return (new, carry)
            init = jnp.zeros((b, h, p, D_STATE), x.dtype)
            _, prevs = jax.lax.scan(step, init, (jnp.moveaxis(states, 1, 0), jnp.moveaxis(chunk_decay, 1, 0)))
            prev_states = jnp.moveaxis(prevs, 0, 1)
            y_inter = jnp.einsum('bcihn,bcih,bchpn->bcihp', Ch, jnp.exp(dA_cs), prev_states)
            return (y_intra + y_inter).reshape(b, l, h, p)
        B, C, H, W = u.shape
        L = H * W
        useq = u.reshape(B, C, L).transpose(0, 2, 1)
        zxbcdt = useq @ in_proj_w.T
        z = zxbcdt[..., :D_INNER]
        xBC = zxbcdt[..., D_INNER:D_INNER + CONV_DIM]
        dt = jax.nn.softplus(zxbcdt[..., D_INNER + CONV_DIM:] + dt_bias)
        xBC = xBC.reshape(B, H, W, CONV_DIM)
        kern = jnp.transpose(conv_w, (2, 3, 1, 0))
        xBC = jax.lax.conv_general_dilated(xBC, kern, (1, 1), 'SAME', dimension_numbers=('NHWC', 'HWIO', 'NHWC'), feature_group_count=CONV_DIM) + conv_b
        xBC = jax.nn.silu(xBC).reshape(B, L, CONV_DIM)
        x = xBC[..., :D_INNER].reshape(B, L, NHEADS, HEADDIM)
        Bm = xBC[..., D_INNER:D_INNER + NGROUPS * D_STATE].reshape(B, L, NGROUPS, D_STATE)
        Cm = xBC[..., D_INNER + NGROUPS * D_STATE:].reshape(B, L, NGROUPS, D_STATE)
        A = -jnp.exp(A_log)
        y = _chunk_scan(x, dt, A, Bm, Cm) + D[None, None, :, None] * x
        y = y.reshape(B, L, D_INNER)
        mu = jnp.mean(y, axis=-1, keepdims=True)
        var = jnp.var(y, axis=-1, keepdims=True)
        y = (y - mu) / jnp.sqrt(var + EPS) * norm_w + norm_b
        y = y * z
        out = y @ out_proj_w.T
        return out.reshape(B, H, W, C).transpose(0, 3, 1, 2)

    def _gn(v, G=32, eps=1e-05):
        B_, C_, H_, W_ = v.shape
        g = v.reshape(B_, G, C_ // G, H_, W_)
        m = jnp.mean(g, axis=(2, 3, 4), keepdims=True)
        s = jnp.var(g, axis=(2, 3, 4), keepdims=True)
        return ((g - m) / jnp.sqrt(s + eps)).reshape(v.shape)

    def _ln_c(v, eps=1e-06):
        m = jnp.mean(v, axis=1, keepdims=True)
        s = jnp.var(v, axis=1, keepdims=True)
        return (v - m) / jnp.sqrt(s + eps)

    def _ln_t(v, eps=1e-05):
        m = jnp.mean(v, axis=-1, keepdims=True)
        s = jnp.var(v, axis=-1, keepdims=True)
        return (v - m) / jnp.sqrt(s + eps)

    def _to_tokens(v):
        B_, C_, H_, W_ = v.shape
        return v.reshape(B_, C_, H_ * W_).transpose(0, 2, 1)

    def _from_tokens(t, like):
        B_, C_, H_, W_ = like.shape
        return t.transpose(0, 2, 1).reshape(B_, C_, H_, W_)
    x = x + _L0_conv_ref(_gn(x), L0_conv_qkv_w, L0_conv_proj_w, L0_conv_proj_b)
    x = x + _L1_conv_ref(_gn(x), L1_conv_x_proj_weight, L1_conv_dt_projs_weight, L1_conv_dt_projs_bias, L1_conv_A_logs, L1_conv_Ds, L1_conv_ln_weight, L1_conv_ln_bias)
    x = x + _L2_conv_ref(_gn(x), L2_conv_weight, L2_conv_bias)
    x = x + _L3_conv_ref(_gn(x), L3_conv_in_proj_w, L3_conv_conv_w, L3_conv_conv_b, L3_conv_dt_bias, L3_conv_A_log, L3_conv_D, L3_conv_norm_w, L3_conv_norm_b, L3_conv_out_proj_w)
    return x

_drawn_inputs = setup_inputs


def setup_inputs(seed=0):
    import zlib

    import numpy as np

    out = dict(_drawn_inputs(seed))
    spreads = {'L1_conv_Ds': (1.0, 0.2),
     'L1_conv_ln_weight': (1.0, 0.2),
     'L1_conv_ln_bias': (0.0, 0.1),
     'L3_conv_D': (1.0, 0.2),
     'L3_conv_norm_w': (1.0, 0.2),
     'L3_conv_norm_b': (0.0, 0.1)}
    factors = {'L0_conv_proj_b': 3.873, 'L3_conv_conv_b': 8.0}
    for name, (base, spread) in spreads.items():
        noise = np.random.default_rng([zlib.crc32(name.encode()), seed]).standard_normal(out[name].shape)
        drawn = base * np.exp(spread * noise) if base else spread * noise
        out[name] = jnp.asarray(drawn.astype(out[name].dtype))
    for name, factor in factors.items():
        out[name] = (out[name] * factor).astype(out[name].dtype)
    return out
```

```python
from contextlib import ExitStack

import concourse.bass as bass
from concourse import mybir

F32 = mybir.dt.float32
BF16 = mybir.dt.bfloat16
ALU = mybir.AluOpType
ACT = mybir.ActivationFunctionType
AX = mybir.AxisListType

B, C, H, W = 16, 192, 32, 32
L = H * W
HALF = 512
CT = [128, C - 128]
HEADS, DH = 6, 32
K, N, R = 4, 16, 6
TOP = 30
NH, HP, NS = 12, 32, 32
DI = NH * HP
ZT = DI // 128
Q = 128
NCH = L // Q
PAD = H + 2
SOFTPLUS_LINEAR = 30.0
REPLACED = -3.0e38

CONSTS = ["ident", "group", "ones", "sel_n", "upper", "head_ones", "sel_head", "unit_row", "mask"]


def consts():
    import numpy as np

    ch = np.arange(C)
    same = (ch[:, None] // 6 == ch[None, :] // 6).astype(np.float32) / 6
    group = np.zeros((128, 2, C), np.float32)
    group[:, 0] = same[:128]
    group[:64, 1] = same[128:]
    row = np.arange(96)[:, None, None] % 32
    blk = np.arange(48)[None, :, None]
    half = np.arange(128)[None, None, :] // 64
    sel_n = np.where(blk < 32, row == blk, row == blk - 32 + 16 * half).astype(np.float32)
    h = np.arange(NH)
    head_ones = np.eye(NH, dtype=np.float32)
    sel_head = (h[:, None] == np.arange(DI)[None, :] // HP).astype(np.float32)
    i = np.arange(128)
    unit = np.zeros((128, 1), np.float32)
    unit[[32, 96]] = 1
    return {
        "ident": np.eye(128, dtype=np.float32),
        "group": group,
        "ones": np.ones((128, 128), np.float32),
        "sel_n": sel_n.reshape(96, 48 * 128),
        "upper": (i[:, None] <= i[None, :]).astype(np.float32),
        "head_ones": head_ones,
        "sel_head": sel_head,
        "unit_row": unit,
        "mask": np.where(i[:, None] <= i[None, :], 0, -1e30).astype(np.float32),
    }


def build(nc, x, out, wq, wk, wv, wp, pb, xpw, dtw, dtb, alog, ds, lnw, lnb, cw, cb, wz, wx, wdt,
          mcw, mcb, dtb3, alog3, d3, nw, nb, wo, ident, group, ones, sel_n, upper, head_ones,
          sel_head, unit_row, mask, n_batch=B, phases=4):
    ctx = ExitStack()
    with ctx:
        def sb(name, shape, dt=F32):
            return ctx.enter_context(nc.sbuf_tensor(name, shape, dt))

        sems = []

        def sem(name):
            s = ctx.enter_context(nc.semaphore(name))
            sems.append(s)
            return s

        c_ident = sb("c_ident", [128, 128])
        c_identb = sb("c_identb", [128, 128], BF16)
        c_group = sb("c_group", [128, 2, C])
        c_ones = sb("c_ones", [128, 128])
        c_mean = sb("c_mean", [128, 128])
        c_sel = sb("c_sel", [128, 48 * 128], BF16)
        c_upper = sb("c_upper", [128, 128])
        c_heads = sb("c_heads", [44, NH])
        c_selhead = sb("c_selhead", [128, K * C])
        c_unit = sb("c_unit", [128, 1])
        c_mask = sb("c_mask", [128, 128], BF16)
        w_q = sb("w_q", [128, 2, 3 * 128])
        w_k = sb("w_k", [128, 2, 3 * 128])
        w_v = sb("w_v", [128, 2, C])
        w_p = sb("w_p", [128, 2, C])
        v_pb = sb("v_pb", [128, 2])
        w_xp = sb("w_xp", [128, 2, K, 2, 102])
        w_dt = c_selhead[:, 0:K * C].rearrange("p (k c) -> p k c", k=K)
        v_dtb = sb("v_dtb", [128, 6])
        v_dtb2 = sb("v_dtb2", [64, K])
        v_na = sb("v_na", [128, 6, N])
        v_ds = sb("v_ds", [128, 6])
        v_lnw = sb("v_lnw", [128, 2])
        v_lnb = sb("v_lnb", [128, 2])
        v_cw = sb("v_cw", [128, 2, 9])
        v_cb = sb("v_cb", [128, 2])
        w_z = sb("w_z", [128, 2, DI])
        w_x = sb("w_x", [128, 2, DI + 2 * NS])
        w_dt3 = sb("w_dt3", [128, 2, NH])
        v_mcw = sb("v_mcw", [128, 4, 9])
        v_mcb = sb("v_mcb", [128, 4])
        v_mcbC = sb("v_mcbC", [32, 1])
        v_dtb3 = sb("v_dtb3", [128, NH])
        v_na3 = sb("v_na3", [128, NH])
        v_d3 = sb("v_d3", [128, ZT])
        v_nw = sb("v_nw", [128, ZT])
        v_nb = sb("v_nb", [128, ZT])
        w_o = sb("w_o", [128, ZT, C])
        diag = sb("diag", [128, 4, 9, 128])
        v_eps5 = sb("v_eps5", [128, 1])

        X = sb("X", [128, 2, L])
        XN = sb("XN", [128, 2, L])
        g_st = sb("g_st", [128, 2, 2, 6])
        g_mv = sb("g_mv", [128, 2, 2])
        g_s = sb("g_s", [128, 2, 2])
        g_t = sb("g_t", [128, 2, 4])

        WORDS = 31400
        arena = sb("arena", [128, WORDS])
        used = [0]

        def area(shape, dt=F32):
            n = 1
            for s in shape:
                n *= s
            words = n if dt == F32 else (n + 1) // 2
            v = arena[:, used[0]:used[0] + words]
            used[0] += words
            assert used[0] <= WORDS, used[0]
            if dt != F32:
                v = v.bitcast(dt)
            if len(shape) > 1:
                names = "abcd"[:len(shape)]
                v = v.rearrange(f"p ({' '.join(names)}) -> p {' '.join(names)}",
                                **{n_: s for n_, s in zip(names[1:], shape[1:])})
            return v

        ps = [ctx.enter_context(nc.psum_tensor(f"ps{i}", [128, L], F32)) for i in range(4)]

        s_ld = sem("weights_loaded")
        s_w = sem("tables_worked_out")
        s_we = sem("exponentials_ready")

        used[0] = 0
        sel_f = area([48 * 128])
        mask_f = area([128])
        with nc.Block() as block:
            loads = []

            def two(dst, src):
                loads.append((dst[0:128, 0], src[0:128]))
                loads.append((dst[0:64, 1], src[128:192]))

            loads += [(c_ident[:], ident), (c_group[:], group), (c_ones[:], ones), (sel_f[0:96, :], sel_n),
                      (c_upper[:], upper), (c_heads[0:NH], head_ones), (c_heads[32:32 + NH], head_ones),
                      (c_selhead[0:NH, 0:DI], sel_head), (c_unit[:], unit_row), (mask_f[:, :], mask)]
            two(w_q, wq)
            two(w_k, wk)
            two(w_v, wv)
            two(w_p, wp)
            two(v_pb, pb)
            two(w_xp, xpw)
            loads.append((w_dt[96:102], dtw))
            for src, dst in ((dtb, v_dtb), (ds, v_ds), (alog, v_na)):
                for t, k in enumerate((0, 2, 1, 3)):
                    loads.append((dst[0:128, t], src[k, 0:128]))
                for t, ks in ((4, (0, 1)), (5, (2, 3))):
                    loads.append((dst[0:64, t], src[ks[0], 128:192]))
                    loads.append((dst[64:128, t], src[ks[1], 128:192]))
            for k in range(K):
                loads.append((v_dtb2[0:64, k], dtb[k, 128:192]))
            two(v_lnw, lnw)
            two(v_lnb, lnb)
            two(v_cw, cw)
            two(v_cb, cb)
            two(w_z, wz)
            two(w_x, wx)
            two(w_dt3, wdt)
            for t in range(4):
                n = min(128, DI + 2 * NS - 128 * t)
                loads.append((v_mcw[0:n, t], mcw[128 * t:128 * t + n]))
                loads.append((v_mcb[0:n, t], mcb[128 * t:128 * t + n]))
            loads.append((v_mcbC[:], mcb[DI + NS:DI + 2 * NS]))
            loads.append((v_dtb3[:], dtb3.partition_broadcast(128)))
            loads.append((v_na3[:], alog3.partition_broadcast(128)))
            for h in range(NH):
                loads.append((v_d3[HP * (h % 4):HP * (h % 4) + HP, h // 4:h // 4 + 1],
                              d3[h:h + 1].partition_broadcast(HP)))
            for t in range(ZT):
                loads.append((v_nw[:, t], nw[128 * t:128 * t + 128]))
                loads.append((v_nb[:, t], nb[128 * t:128 * t + 128]))
                loads.append((w_o[:, t], wo[128 * t:128 * t + 128]))

            @block.sync
            def _(sp):
                for dst, src in loads:
                    if len(dst.shape) < len(src.shape):
                        dst = dst.unsqueeze(len(dst.shape))
                    if len(src.shape) < len(dst.shape):
                        src = src.unsqueeze(len(src.shape))
                    sp.dma_start(dst, src).then_inc(s_ld, 16)

            @block.scalar
            def _(act):
                act.wait_ge(s_ld, 16 * len(loads))
                nc.scalar.activation(v_na[:], v_na[:], ACT.Exp).then_inc(s_we, 1)
                nc.scalar.activation(v_na3[:], v_na3[:], ACT.Exp).then_inc(s_we, 1)

            @block.vector
            def _(dve):
                dve.wait_ge(s_ld, 16 * len(loads))
                nc.vector.tensor_copy(c_identb[:], c_ident[:]).then_inc(s_w, 1)
                nc.vector.tensor_copy(c_sel[0:96], sel_f[0:96, :]).then_inc(s_w, 1)
                nc.vector.tensor_copy(c_mask[:], mask_f[:, :]).then_inc(s_w, 1)
                nc.vector.tensor_scalar(c_mean[:], c_ones[:], 1.0 / C, None, ALU.mult).then_inc(s_w, 1)
                nc.vector.memset(v_eps5[:], 1e-5).then_inc(s_w, 1)
                for t in range(4):
                    n = min(128, DI + 2 * NS - 128 * t)
                    for tap in range(9):
                        nc.vector.tensor_scalar(diag[0:n, t, tap, 0:n], c_ident[0:n, 0:n], v_mcw[0:n, t, tap:tap + 1],
                                                None, ALU.mult).then_inc(s_w, 1)
                dve.wait_ge(s_we, 2)
                nc.vector.tensor_scalar(v_na[:], v_na[:], -1.0, None, ALU.mult).then_inc(s_w, 1)
                nc.vector.tensor_scalar(v_na3[:], v_na3[:], -1.0, None, ALU.mult).then_inc(s_w, 1)

        g_stat = sem("group_stats_ready")
        g_sum = sem("group_sums_ready")
        g_var = sem("group_var_ready")
        g_std = sem("group_std_ready")
        g_dve = sem("group_norm_dve_steps")
        g_xn = sem("normalised_ready")

        def norm_dve(dve, u, writes):
            base = 10 * u
            k = 0
            for t, n in enumerate(CT):
                for h in range(2):
                    nc.vector.bn_stats(g_st[0:n, t, h, :], X[0:n, t, HALF * h:HALF * h + HALF]).then_inc(g_dve, 1)
                    k += 1
                dve.wait_ge(g_dve, base + k)
                nc.vector.bn_aggr(g_mv[0:n, t, :], g_st[0:n, t, :, :]).then_inc(g_dve, 1)
                k += 1
            dve.wait_ge(g_dve, base + k)
            for t, n in enumerate(CT):
                nc.vector.tensor_copy(g_s[0:n, t, 0:1], g_mv[0:n, t, 0:1]).then_inc(g_stat, 1)
                nc.vector.scalar_tensor_tensor(g_s[0:n, t, 1:2], g_mv[0:n, t, 0:1], g_mv[0:n, t, 0:1],
                                               g_mv[0:n, t, 1:2], ALU.mult, ALU.add).then_inc(g_stat, 1)
            dve.wait_ge(g_sum, u + 1)
            for t, n in enumerate(CT):
                p = ps[0][0:n, 8 * t:8 * t + 2]
                nc.vector.tensor_copy(g_t[0:n, t, 0:2], p).then_inc(g_dve, 1)
                k += 1
            dve.wait_ge(g_dve, base + k)
            for t, n in enumerate(CT):
                nc.vector.tensor_tensor(g_t[0:n, t, 2:3], g_t[0:n, t, 0:1], g_t[0:n, t, 0:1], ALU.mult).then_inc(g_dve, 1)
                k += 1
            dve.wait_ge(g_dve, base + k)
            assert k == 10
            for t, n in enumerate(CT):
                nc.vector.tensor_tensor(g_t[0:n, t, 2:3], g_t[0:n, t, 1:2], g_t[0:n, t, 2:3],
                                        ALU.subtract).then_inc(g_var, 1)
            dve.wait_ge(g_std, 2 * u + 2)
            for t, n in enumerate(CT):
                nc.vector.reciprocal(g_t[0:n, t, 2:3], g_t[0:n, t, 3:4]).then_inc(g_var, 1)
            dve.wait_ge(g_var, 4 * u + 4)
            for t, n in enumerate(CT):
                src = X[0:n, t, :]
                dst = writes(t, n)
                if len(dst.shape) == 3:
                    src = src.rearrange("p (h w) -> p h w", w=W)
                nc.vector.tensor_scalar(dst, src, g_t[0:n, t, 0:1], g_t[0:n, t, 2:3], ALU.subtract,
                                        ALU.mult).then_inc(g_xn, 1)

        def norm_pe(pe, u):
            pe.wait_ge(g_stat, 4 * u + 4)
            for t, n in enumerate(CT):
                for s, m in enumerate(CT):
                    mm = nc.tensor.matmul(ps[0][0:n, 8 * t:8 * t + 2], c_group[0:m, s, 128 * t:128 * t + n],
                                          g_s[0:m, s, :], start=(s == 0), stop=(s == 1))
            mm.then_inc(g_sum, 1)

        def norm_act(act, u):
            for t, n in enumerate(CT):
                act.wait_ge(g_var, 4 * u + t + 1)
                nc.scalar.activation(g_t[0:n, t, 3:4], g_t[0:n, t, 2:3], ACT.Sqrt, bias=v_eps5[0:n, :]).then_inc(g_std, 1)

        s_x = sem("image_loaded")
        s_out = sem("image_stored")

        used[0] = 0
        QA = area([3, L])
        KA = area([3, L])
        QB = area([3, L], BF16)
        KB = area([3, L], BF16)
        V = area([NCH, HEADS, 64])
        MX = area([HEADS * NCH])
        PT = area([3, L])
        OA = area([2, L])
        RD = area([2, L])

        a_qk = sem("attn_qk_psum_ready")
        a_qkc = sem("attn_qk_copied")
        a_v = sem("attn_v_psum_ready")
        a_vc = sem("attn_v_copied")
        a_s = sem("attn_rough_scores_ready")
        a_m = sem("attn_row_max_ready")
        a_r = sem("attn_max_rows_ready")
        a_rc = sem("attn_max_rows_copied")
        a_st = sem("attn_scores_ready")
        a_e = sem("attn_exp_ready")
        a_pv = sem("attn_exp_used")
        a_rd = sem("attn_denominators_inverted")
        a_o = sem("attn_heads_ready")
        a_p = sem("attn_projection_ready")
        a_x = sem("attn_added")

        def attn_pe(pe):
            pe.wait_ge(g_xn, 2)
            for i in range(6):
                w, t = (w_q, w_k)[i % 2], i // 2
                if i >= 2:
                    pe.wait_ge(a_qkc, 2 * (i - 1))
                for h in range(2):
                    for c, m in enumerate(CT):
                        mm = nc.tensor.matmul(ps[i % 2][:, HALF * h:HALF * h + HALF], w[0:m, c, 128 * t:128 * t + 128],
                                              XN[0:m, c, HALF * h:HALF * h + HALF], start=(c == 0), stop=(c == 1))
                mm.then_inc(a_qk, 1)
            for j in range(NCH):
                for c, m in enumerate(CT):
                    mm = nc.tensor.matmul(ps[2 + j // 4][:, 256 * (j % 4):256 * (j % 4) + C],
                                          XN[0:m, c, Q * j:Q * j + Q], w_v[0:m, c, :], start=(c == 0), stop=(c == 1))
                if j % 4 == 3:
                    mm.then_inc(a_v, 1)
            for h in range(HEADS):
                t, r = h // 2, 64 * (h % 2)
                for j in range(NCH):
                    i = NCH * h + j
                    if i == 0:
                        pe.wait_ge(a_qkc, 12)
                    if i >= 2:
                        pe.wait_ge(a_m, i - 1)
                    for m in range(2):
                        mm = nc.tensor.matmul(ps[i % 2][:, HALF * m:HALF * m + HALF], QB[r:r + DH, t, Q * j:Q * j + Q],
                                              KB[r:r + DH, t, HALF * m:HALF * m + HALF], start=True, stop=True)
                    mm.then_inc(a_s, 1)
            pe.wait_ge(a_vc, 2)
            pe.wait_ge(a_m, HEADS * NCH)
            for h in range(HEADS):
                t, r = h // 2, 64 * (h % 2) + 32
                if h >= 4:
                    pe.wait_ge(a_rc, h - 3)
                for j in range(NCH):
                    mm = nc.tensor.matmul(ps[t % 2 + 2][r:r + 1, Q * j:Q * j + Q], MX[:, NCH * h + j:NCH * h + j + 1],
                                          c_ident[:], start=True, stop=True)
                mm.then_inc(a_r, 1)
            n = HEADS * NCH
            for i in range(n + 1):
                if i < n:
                    h, j = i // NCH, i % NCH
                    t, r = h // 2, 64 * (h % 2)
                    pe.wait_ge(a_rc, h + 1)
                    if i >= 2:
                        pe.wait_ge(a_e, i - 1)
                    for m in range(2):
                        mm = nc.tensor.matmul(ps[i % 2][:, HALF * m:HALF * m + HALF], KA[r:r + DH + 1, t, Q * j:Q * j + Q],
                                              QA[r:r + DH + 1, t, HALF * m:HALF * m + HALF], start=True, stop=True)
                    mm.then_inc(a_st, 1)
                if i > 0:
                    h, j = (i - 1) // NCH, (i - 1) % NCH
                    t, r = h // 2, 64 * (h % 2)
                    if j == 0 and h % 2 == 0 and t == 0:
                        pe.wait_ge(a_rc, HEADS)
                    if j == 0 and h % 2 == 0 and t == 2:
                        pe.wait_ge(a_o, 2)
                    pe.wait_ge(a_e, i)
                    for m in range(2):
                        mm = nc.tensor.matmul(ps[2 + t % 2][r:r + 64, HALF * m:HALF * m + HALF], V[:, j, h, :],
                                              PT[:, (i - 1) % 3, HALF * m:HALF * m + HALF], start=(j == 0), stop=(j == NCH - 1))
                    mm.then_inc(a_pv, 1)
            pe.wait_ge(a_o, HEADS)
            for o, n in enumerate(CT):
                for m in range(2):
                    for c, kk in enumerate(CT):
                        mm = nc.tensor.matmul(ps[o][0:n, HALF * m:HALF * m + HALF], w_p[0:kk, c, 128 * o:128 * o + n],
                                              OA[0:kk, c, HALF * m:HALF * m + HALF], start=(c == 0), stop=(c == 1))
                mm.then_inc(a_p, 1)

        def attn_act(act):
            for i in range(6):
                t = i // 2
                act.wait_ge(a_qk, i + 1)
                if i % 2 == 0:
                    nc.scalar.activation(QA[:, t, :], ps[0][:], ACT.Copy).then_inc(a_qkc, 1)
                    nc.scalar.activation(QB[:, t, :], ps[0][:], ACT.Copy).then_inc(a_qkc, 1)
                else:
                    nc.scalar.activation(KA[:, t, :], ps[1][:], ACT.Identity, bias=c_unit[:]).then_inc(a_qkc, 1)
                    nc.scalar.activation(KB[:, t, :], ps[1][:], ACT.Copy).then_inc(a_qkc, 1)
            for g in range(2):
                act.wait_ge(a_v, g + 1)
                nc.scalar.activation(V[:, 4 * g:4 * g + 4, :, 0:DH],
                                     ps[2 + g][:].rearrange("p (j c) -> p j c", j=4)[:, :, 0:C].rearrange(
                                         "p j (h d) -> p j h d", d=DH), ACT.Copy).then_inc(a_vc, 1)
            for h in range(HEADS):
                t, r = h // 2, 64 * (h % 2) + 32
                act.wait_ge(a_r, h + 1)
                nc.scalar.activation(QA[r:r + 1, t, :], ps[t % 2 + 2][r:r + 1, :], ACT.Copy, scale=-1.0).then_inc(a_rc, 1)
            for i in range(HEADS * NCH):
                act.wait_ge(a_st, i + 1)
                if i >= 3:
                    act.wait_ge(a_pv, i - 2)
                nc.scalar.activation(PT[:, i % 3, :], ps[i % 2][:], ACT.Exp, scale=DH ** -0.5).then_inc(a_e, 1)

        def attn_dve(dve):
            for i in range(HEADS * NCH):
                dve.wait_ge(a_s, i + 1)
                nc.vector.reduce_max(MX[:, i:i + 1], ps[i % 2][:], AX.X).then_inc(a_m, 1)
            for t in range(3):
                dve.wait_ge(a_pv, 2 * NCH * (t + 1))
                O = ps[2 + t % 2]
                for e in range(2):
                    h, r = 2 * t + e, 64 * e
                    nc.vector.reciprocal(RD[r + 32:r + 64, t % 2, :], O[r + 32:r + 64, :]).then_inc(a_rd, 1)
                for e in range(2):
                    h, r = 2 * t + e, 64 * e
                    dve.wait_ge(a_rd, h + 1)
                    nc.vector.tensor_tensor(OA[DH * (h % 4):DH * (h % 4) + DH, h // 4, :], O[r:r + 32, :],
                                            RD[r + 32:r + 64, t % 2, :], ALU.mult).then_inc(a_o, 1)
            for o, n in enumerate(CT):
                dve.wait_ge(a_p, o + 1)
                nc.vector.scalar_tensor_tensor(X[0:n, o, :], ps[o][0:n, :], v_pb[0:n, o:o + 1], X[0:n, o, :],
                                               ALU.add, ALU.add).then_inc(a_x, 1)

        used[0] = 0
        XT = area([2, L])
        UM = XN[:, 1, :]
        DT = area([6, L])
        DU = area([6, L])
        BC = area([K, L], BF16)
        RES = area([L])
        DG = area([6, 128])
        DRK = RES
        dA = area([2, L])
        MID = dA[:, 0, 0:L // 2].bitcast(BF16)
        bu = area([2, L])
        hs = area([2, L])
        Cs = area([2, L])
        hc = area([2, L])
        YA = area([2, L])
        SP = YA[:, 1, :]
        YS = SP
        assert used[0] < WORDS
        TILE_K = [(0,), (2,), (1,), (3,), (0, 1), (2, 3)]
        GROUPS = [(0, 1), (2, 3), (4, 5)]

        m_t = sem("scan_inputs_ready")
        m_xd = sem("scan_xdbl_ready")
        m_hi = sem("scan_high_parts_ready")
        m_r = sem("scan_rests_ready")
        m_mid = sem("scan_middle_parts_ready")
        m_bc = sem("scan_bc_ready")
        m_dtp = sem("scan_dt_psum_ready")
        m_cl = sem("scan_dt_clamped")
        m_e = sem("scan_dt_exp")
        m_ln = sem("scan_dt_log")
        m_dt = sem("scan_dt_ready")
        m_du = sem("scan_dtu_ready")
        m_dg = sem("scan_diagonals_ready")
        m_b = [sem(f"scan_b_rows_{g}") for g in range(3)]
        m_c = [sem(f"scan_c_rows_{g}") for g in range(3)]
        m_cc = [sem(f"scan_c_copied_{g}") for g in range(3)]
        m_da = [sem(f"scan_decay_{g}") for g in range(3)]
        m_bu = [sem(f"scan_input_{g}") for g in range(3)]
        m_h = [sem(f"scan_state_{g}") for g in range(3)]
        m_hc = [sem(f"scan_product_{g}") for g in range(3)]
        m_y = [sem(f"scan_product_summed_{g}") for g in range(3)]
        m_yd = sem("scan_group_summed")
        m_yc = sem("scan_group_copied")
        m_ys = sem("scan_y_ready")
        m_mu = sem("scan_mean_ready")
        m_ce = sem("scan_centred")
        m_sq = sem("scan_squares_ready")
        m_va = sem("scan_var_ready")
        m_sd = sem("scan_std_ready")
        m_rs = sem("scan_rstd_ready")
        m_n = sem("scan_normalised")
        m_ge = sem("scan_gelu_ready")
        m_x = sem("scan_added")

        def source(t):
            return (XN[:, 0, :], XN[:, 0, :], XT[:, 0, :], XT[:, 0, :], UM, UM)[t]

        def scan_pe(pe):
            pe.wait_ge(g_xn, 4)
            pe.wait_ge(m_t, 2)
            for k in range(K):
                P = ps[k % 2]
                if k >= 2:
                    pe.wait_ge(m_bc, k - 1)
                for h in range(2):
                    for o, src in enumerate((XN, XT)):
                        for c, m in enumerate(CT):
                            mm = nc.tensor.matmul(P[0:102, HALF * h:HALF * h + HALF], w_xp[0:m, c, k, o, :],
                                                  src[0:m, c, HALF * h:HALF * h + HALF], start=(o == 0 and c == 0),
                                                  stop=(o == 1 and c == 1))
                mm.then_inc(m_xd, 1)
                pe.wait_ge(m_hi, 2 * (k + 1))
                if k >= 1:
                    pe.wait_ge(m_dt, 2 * k)
                for h in range(2):
                    for c, m in enumerate(CT):
                        mm = nc.tensor.matmul(ps[2 + c][0:m, HALF * h:HALF * h + HALF], w_dt[96:102, k, 128 * c:128 * c + m],
                                              DRK[96:102, HALF * h:HALF * h + HALF], start=True, stop=True)
                mm.then_inc(m_dtp, 1)
            pe.wait_ge(m_bc, K)
            pe.wait_ge(m_dt, 2 * K)
            pe.wait_ge(m_dg, 6)
            pe.wait_ge(m_t, 3)
            def rows(g, t, e, n):
                for j, P in enumerate((ps[e], ps[2])):
                    if j == 0:
                        pe.wait_ge(m_bu[g], 2 * n + (e + 1))
                    else:
                        pe.wait_ge(m_cc[g], 2 * n + (e + 1))
                    if t < 4:
                        k = TILE_K[t][0]
                        at = n * 128 + 128 * 16 * (k % 2)
                    else:
                        k = TILE_K[t][0]
                        at = n * 128 + 128 * 32
                    at = slice(at, at + 128) if isinstance(n, int) else bass.ds(at, 128)
                    for h in range(2):
                        mm = nc.tensor.matmul(P[:, HALF * h:HALF * h + HALF], c_sel[0:96, at],
                                              BC[0:96, 2 * (k // 2) + j, HALF * h:HALF * h + HALF],
                                              start=True, stop=True)
                    mm.then_inc((m_b, m_c)[j][g], 1)

            def add(g, e, n):
                pe.wait_ge(m_hc[g], 2 * n + (e + 3))
                for h in range(2):
                    mm = nc.tensor.matmul(ps[3][:, HALF * h:HALF * h + HALF], c_ident[:],
                                          hc[:, e, HALF * h:HALF * h + HALF], start=False, stop=False,
                                          skip_group_check=True)
                mm.then_inc(m_y[g], 1)

            for g, tiles in enumerate(GROUPS):
                Y = ps[3]
                pe.sem_inc(m_y[g], 2)
                if g > 0:
                    pe.wait_ge(m_yc, g)
                for h in range(2):
                    nc.tensor.matmul(Y[:, HALF * h:HALF * h + HALF], DG[:, tiles[0], :],
                                     source(tiles[0])[:, HALF * h:HALF * h + HALF], start=True, stop=False,
                                     skip_group_check=True)
                for e, t in enumerate(tiles):
                    rows(g, t, e, 0)
                with pe.Fori(1, N) as n:
                    for e, t in enumerate(tiles):
                        rows(g, t, e, n)
                        add(g, e, n - 1)
                for e, t in enumerate(tiles):
                    add(g, e, N - 1)
                for h in range(2):
                    mm = nc.tensor.matmul(Y[:, HALF * h:HALF * h + HALF], DG[:, tiles[1], :],
                                          source(tiles[1])[:, HALF * h:HALF * h + HALF], start=False, stop=True,
                                          skip_group_check=True)
                mm.then_inc(m_yd, 1)
            for src, ready, done, P in ((YA, m_ys, m_mu, ps[0]), (None, m_sq, m_va, ps[1])):
                pe.wait_ge(ready, 2)
                if src is None:
                    src = hs
                for h in range(2):
                    for c, m in enumerate(CT):
                        mm = nc.tensor.matmul(P[:, HALF * h:HALF * h + HALF], c_mean[0:m, :],
                                              src[0:m, c, HALF * h:HALF * h + HALF], start=(c == 0), stop=(c == 1))
                mm.then_inc(done, 1)

        def scan_act(act):
            for c, m in enumerate(CT):
                act.wait_ge(g_xn, 3 + c)
                nc.scalar.activation(XT[0:m, c, :].rearrange("p (w h) -> p w h", h=H),
                                     XN[0:m, c, :].rearrange("p (h w) -> p w h", w=W), ACT.Copy).then_inc(m_t, 1)
            act.wait_ge(m_t, 2)
            nc.scalar.activation(UM[64:128, :], XT[0:64, 1, :], ACT.Copy).then_inc(m_t, 1)
            for k in range(K):
                P = ps[k % 2]
                act.wait_ge(m_xd, k + 1)
                if k >= 1:
                    act.wait_ge(m_dtp, k)
                nc.scalar.activation(DRK[96:102, :], P[96:102, :], ACT.Copy).then_inc(m_hi, 1)
                nc.scalar.activation(BC[0:96, k, :], P[0:96, :], ACT.Copy).then_inc(m_hi, 1)
                act.wait_ge(m_r, k + 1)
                nc.scalar.activation(BC[32:64, k, :], RES[32:64, :], ACT.Copy).then_inc(m_mid, 1)
                nc.scalar.activation(MID[64:96, :], RES[64:96, :], ACT.Copy).then_inc(m_mid, 1)
                for c in range(2):
                    i = 2 * k + c
                    t, rows = dt_place(k, c)
                    act.wait_ge(m_cl, i + 1)
                    nc.scalar.activation(SP[rows, :], SP[rows, :], ACT.Exp).then_inc(m_e, 1)
                    act.wait_ge(m_e, i + 1)
                    nc.scalar.activation(SP[rows, :], SP[rows, :], ACT.Ln, bias=1.0).then_inc(m_ln, 1)
            act.wait_ge(m_dt, 2 * K)
            for g, tiles in enumerate(GROUPS):
                act.sem_inc(m_cc[g], 1)
                with act.Fori(0, N) as n:
                    for e, t in enumerate(tiles):
                        act.wait_ge(m_h[g], 2 * n + (e + 1))
                        nc.scalar.activation(dA[:, e, :], DT[:, t, :], ACT.Exp,
                                             scale=v_na[:, t, bass.ds(n, 1)]).then_inc(m_da[g], 1)
                        act.wait_ge(m_c[g], 2 * n + (e + 1))
                        act.wait_ge(m_hc[g], 2 * n + (e + 1))
                        nc.scalar.activation(Cs[:, e, :], ps[2][:], ACT.Copy).then_inc(m_cc[g], 1)
                act.wait_ge(m_yd, g + 1)
                if g == 0:
                    nc.scalar.activation(YA[:, 0, :], ps[3][:], ACT.Copy).then_inc(m_yc, 1)
                elif g == 1:
                    nc.scalar.activation(YS[:, :], ps[3][:], ACT.Copy).then_inc(m_yc, 1)
                else:
                    nc.scalar.activation(YA[0:64, 1, :], ps[3][0:64, :], ACT.Copy).then_inc(m_yc, 1)
                    nc.scalar.activation(RES[0:64, :], ps[3][64:128, :], ACT.Copy).then_inc(m_yc, 1)
            for c, m in enumerate(CT):
                act.wait_ge(m_ce, c + 1)
                nc.scalar.activation(hs[0:m, c, :], YA[0:m, c, :], ACT.Square).then_inc(m_sq, 1)
            act.wait_ge(m_va, 1)
            nc.scalar.activation(RES[:, :], ps[1][:], ACT.Sqrt, bias=v_eps5[:]).then_inc(m_sd, 1)
            for c, m in enumerate(CT):
                act.wait_ge(m_n, c + 1)
                nc.scalar.activation(YA[0:m, c, :], YA[0:m, c, :], ACT.Gelu, bias=v_lnb[0:m, c:c + 1],
                                     scale=v_lnw[0:m, c:c + 1]).then_inc(m_ge, 1)

        def dt_place(k, c):
            if c == 0:
                return (0, 2, 1, 3)[k], slice(0, 128)
            return 4 + k // 2, slice(64 * (k % 2), 64 * (k % 2) + 64)

        def scan_dve(dve):
            for k in range(K):
                P = ps[k % 2]
                dve.wait_ge(m_hi, 2 * (k + 1))
                if k >= 1:
                    dve.wait_ge(m_mid, 2 * k)
                nc.vector.tensor_tensor(RES[0:96, :], P[0:96, :], BC[0:96, k, :], ALU.subtract).then_inc(m_r, 1)
                dve.wait_ge(m_r, k + 1)
                dve.wait_ge(m_mid, 2 * (k + 1))
                nc.vector.tensor_tensor(BC[64:96, k, :], RES[64:96, :], MID[64:96, :], ALU.subtract).then_inc(m_bc, 1)
                dve.wait_ge(m_dtp, k + 1)
                for c, m in enumerate(CT):
                    i = 2 * k + c
                    t, rows = dt_place(k, c)
                    if i > 0:
                        dve.wait_ge(m_dt, i)
                    nc.vector.tensor_scalar(SP[rows, :], ps[2 + c][0:m, :], v_dtb[rows, t:t + 1] if c == 0 else
                                            v_dtb2[0:m, k:k + 1], SOFTPLUS_LINEAR, ALU.add, ALU.min).then_inc(m_cl, 1)
                    dve.wait_ge(m_ln, i + 1)
                    nc.vector.scalar_tensor_tensor(DT[rows, t, :], ps[2 + c][0:m, :], v_dtb[rows, t:t + 1] if c == 0 else
                                                   v_dtb2[0:m, k:k + 1], SP[rows, :], ALU.add, ALU.max).then_inc(m_dt, 1)
            for t in range(6):
                nc.vector.tensor_scalar(DG[:, t, :], c_ident[:], v_ds[:, t:t + 1], None, ALU.mult).then_inc(m_dg, 1)
            dve.wait_ge(m_du, 6)
            for g, tiles in enumerate(GROUPS):
                dve.sem_inc(m_bu[g], 2)
                dve.sem_inc(m_h[g], 2)
                with dve.Fori(0, N) as n:
                    for e, t in enumerate(tiles):
                        dve.wait_ge(m_b[g], 2 * n + (e + 1))
                        dve.wait_ge(m_h[g], 2 * n + (e + 1))
                        nc.vector.tensor_tensor(bu[:, e, :], DU[:, t, :], ps[e][:], ALU.mult).then_inc(m_bu[g], 1)
                        dve.wait_ge(m_bu[g], 2 * n + (e + 3))
                        dve.wait_ge(m_da[g], 2 * n + (e + 1))
                        dve.wait_ge(m_hc[g], 2 * n + (e + 1))
                        o = slice(None, None, -1) if e == 1 else slice(None)
                        nc.vector.tensor_tensor_scan(hs[:, e, o], dA[:, e, o], bu[:, e, o], 0.0, ALU.mult,
                                                     ALU.add).then_inc(m_h[g], 1)
                if g == 1:
                    dve.wait_ge(m_yc, 2)
                    nc.vector.tensor_tensor(YA[:, 0, :].rearrange("p (h w) -> p h w", w=W), YA[:, 0, :].rearrange(
                        "p (h w) -> p h w", w=W), YS[:, :].rearrange("p (w h) -> p h w", h=H), ALU.add).then_inc(m_ys, 1)
            dve.wait_ge(m_yc, 4)
            nc.vector.tensor_tensor(YA[0:64, 1, :].rearrange("p (h w) -> p h w", w=W), YA[0:64, 1, :].rearrange(
                "p (h w) -> p h w", w=W), RES[0:64, :].rearrange("p (w h) -> p h w", h=H), ALU.add).then_inc(m_ys, 1)
            dve.wait_ge(m_mu, 1)
            for c, m in enumerate(CT):
                nc.vector.tensor_tensor(YA[0:m, c, :], YA[0:m, c, :], ps[0][0:m, :], ALU.subtract).then_inc(m_ce, 1)
            dve.wait_ge(m_sd, 1)
            nc.vector.reciprocal(RES[:, :], RES[:, :]).then_inc(m_rs, 1)
            dve.wait_ge(m_rs, 1)
            for c, m in enumerate(CT):
                nc.vector.tensor_tensor(YA[0:m, c, :], YA[0:m, c, :], RES[0:m, :], ALU.mult).then_inc(m_n, 1)
            for c, m in enumerate(CT):
                dve.wait_ge(m_ge, c + 1)
                nc.vector.tensor_tensor(X[0:m, c, :], X[0:m, c, :], YA[0:m, c, :], ALU.add).then_inc(m_x, 1)

        def scan_pool(pool):
            pool.wait_ge(m_t, 3)
            pool.wait_ge(m_dt, 2 * K)
            for t in range(6):
                pool.tensor_tensor(DU[:, t, :], DT[:, t, :], source(t), ALU.mult).then_inc(m_du, 1)
            for g in range(3):
                pool.sem_inc(m_hc[g], 2)
                with pool.Fori(0, N) as n:
                    for e in range(2):
                        pool.wait_ge(m_h[g], 2 * n + (e + 3))
                        pool.wait_ge(m_cc[g], 2 * n + (e + 2))
                        pool.wait_ge(m_y[g], 2 * n + (e + 1))
                        pool.tensor_tensor(hc[:, e, :], hs[:, e, :], Cs[:, e, :], ALU.mult).then_inc(m_hc[g], 1)

        used[0] = 0
        XP = area([2, PAD * PAD])
        CD = area([2, 9, 128])
        S = [area([2, L]) for _ in range(2)]
        M8 = area([2, 5, 8])
        XPv = XP.rearrange("p t (h w) -> p t h w", w=PAD)

        k_z = sem("conv_border_cleared")
        k_cd = sem("conv_taps_ready")
        k_s = sem("conv_psum_ready")
        k_sc = sem("conv_scores_ready")
        k_m = sem("topk_steps")
        k_x = sem("conv_added")

        def conv_pe(pe):
            pe.wait_ge(g_xn, 6)
            pe.wait_ge(k_z, 1)
            pe.wait_ge(k_cd, 18)
            for t, n in enumerate(CT):
                for h in range(2):
                    for tap in range(9):
                        dy, dx = tap // 3, tap % 3
                        mm = nc.tensor.matmul(ps[1 + t][0:n, HALF * h:HALF * h + HALF], CD[0:n, t, tap, 0:n],
                                              XPv[0:n, t, dy + 16 * h:dy + 16 * h + 16, dx:dx + W],
                                              start=(tap == 0), stop=(tap == 8))
                mm.then_inc(k_s, 1)

        def conv_act(act):
            for t, n in enumerate(CT):
                act.wait_ge(k_s, t + 1)
                nc.scalar.activation(S[0][0:n, t, :], ps[1 + t][0:n, :], ACT.Identity,
                                     bias=v_cb[0:n, t:t + 1]).then_inc(k_sc, 1)

        def conv_pool(pool):
            pool.wait_ge(m_x, 2)
            pool.memset(XP[:, :, :], 0.0).then_inc(k_z, 1)
            for t, n in enumerate(CT):
                for tap in range(9):
                    pool.tensor_scalar(CD[0:n, t, tap, 0:n], c_ident[0:n, 0:n], v_cw[0:n, t, tap:tap + 1], 1.0,
                                       ALU.mult, ALU.mult).then_inc(k_cd, 1)

        def conv_dve(dve):
            k = 0

            def step(ins):
                nonlocal k
                ins.then_inc(k_m, 1)
                k += 1
                dve.wait_ge(k_m, k)

            for t, n in enumerate(CT):
                dve.wait_ge(k_sc, t + 1)
                rounds = -(-TOP // 8)
                for r in range(rounds):
                    step(nc.vector.max(M8[0:n, t, r, :], S[r % 2][0:n, t, :]))
                    left = TOP - 8 * r
                    if left < 8:
                        step(nc.vector.memset(M8[0:n, t, r, left:8], REPLACED))
                    step(nc.vector.match_replace(S[(r + 1) % 2][0:n, t, :], M8[0:n, t, r, :], S[r % 2][0:n, t, :], REPLACED))
                step(nc.vector.scalar_tensor_tensor(
                    S[1][0:n, t, :].rearrange("p (h w) -> p h w", w=W), S[0][0:n, t, :].rearrange("p (h w) -> p h w", w=W),
                    REPLACED, XPv[0:n, t, 1:1 + H, 1:1 + W], ALU.is_equal, ALU.mult))
                nc.vector.tensor_tensor(X[0:n, t, :], X[0:n, t, :], S[1][0:n, t, :], ALU.add).then_inc(k_x, 1)

        used[0] = 0
        Z = area([ZT, L])
        CP = area([4, PAD * PAD])
        CPv = CP.rearrange("p t (h w) -> p t h w", w=PAD)
        XC = area([ZT, L])
        Bn = area([L])
        Cn = area([L])
        dtT = area([NCH, NH])
        e_t = area([NCH * NH])
        dAT = area([NCH * NH])
        csr = area([L])
        csl = area([L])
        cst = area([NCH * NH])
        dte = area([NCH * NH])
        dec = area([NCH * NH])
        XDT = area([2, DI])
        XW = area([2, DI])
        BT = area([2, NS])
        csb = area([2, NH * Q])
        EX = area([2, NH * Q])
        prev = area([2, DI])
        st_t = area([DI])
        ECS = area([2, DI])
        t1 = area([DI])
        Yn = CP.rearrange("p t l -> p (t l)")[:, 0:ZT * L].rearrange("p (t l) -> p t l", l=L)
        SQ = XC

        b_z = sem("mix_border_cleared")
        b_zp = sem("mix_inproj_psum_ready")
        b_zc = sem("mix_inproj_copied")
        b_cp = sem("mix_conv_psum_ready")
        b_si = sem("mix_silu_ready")
        b_dp = sem("mix_dt_psum_ready")
        b_d1 = sem("mix_dt_biased")
        b_d2 = sem("mix_dt_clamped")
        b_d3 = sem("mix_dt_softplus")
        b_dt = sem("mix_dt_ready")
        b_da = sem("mix_da_ready")
        b_cs = sem("mix_cumsum_psum_ready")
        b_csc = sem("mix_cumsum_copied")
        b_dif = sem("mix_decay_exponent")
        b_dec = sem("mix_decays_ready")
        b_tr = sem("mix_tokens_psum_ready")
        b_bt = sem("mix_b_tokens_copied")
        b_xdt = sem("mix_xdt_ready")
        b_xw = sem("mix_weighted_x_ready")
        b_csb = sem("mix_cumsum_blocks_ready")
        b_ex = sem("mix_exponents_psum_ready")
        b_exc = sem("mix_exp_ready")
        b_g = sem("mix_cb_psum_ready")
        b_att = sem("mix_att_ready")
        b_y = sem("mix_chunk_psum_ready")
        b_ec = sem("mix_inter_decay_ready")
        b_y1 = sem("mix_inter_scaled")
        b_yc = sem("mix_chunk_ready")
        b_pd = sem("mix_state_decayed")
        b_pr = sem("mix_state_ready")
        b_yx = sem("mix_skip_added")
        b_mu = sem("mix_mean_ready")
        b_ce = sem("mix_centred")
        b_sq = sem("mix_squares_ready")
        b_va = sem("mix_var_ready")
        b_sd = sem("mix_std_ready")
        b_rs = sem("mix_rstd_ready")
        b_n1 = sem("mix_scaled")
        b_gz = sem("mix_gated")
        b_o = sem("mix_outproj_ready")
        b_x = sem("mix_added")

        def mix_pe(pe):
            pe.wait_ge(g_xn, 8)
            for i in range(7):
                w, lo, n = (w_z, 128 * i, 128) if i < 3 else (w_x, 128 * (i - 3), 128 if i < 6 else 64)
                if i >= 2:
                    pe.wait_ge(b_zc, i - 1)
                for h in range(2):
                    for c, m in enumerate(CT):
                        mm = nc.tensor.matmul(ps[i % 2][0:n, HALF * h:HALF * h + HALF], w[0:m, c, lo:lo + n],
                                              XN[0:m, c, HALF * h:HALF * h + HALF], start=(c == 0), stop=(c == 1))
                mm.then_inc(b_zp, 1)
            for j in range(NCH):
                for c, m in enumerate(CT):
                    mm = nc.tensor.matmul(ps[2][:, NH * j:NH * j + NH], XN[0:m, c, Q * j:Q * j + Q], w_dt3[0:m, c, :],
                                          start=(c == 0), stop=(c == 1))
            mm.then_inc(b_dp, 1)
            for t in range(4):
                n = 128 if t < 3 else 64
                pe.wait_ge(b_zc, 4 + t)
                if t == 0:
                    pe.wait_ge(b_zc, 7)
                if t >= 2:
                    pe.wait_ge(b_si, t - 1)
                for h in range(2):
                    for tap in range(9):
                        dy, dx = tap // 3, tap % 3
                        mm = nc.tensor.matmul(ps[t % 2][0:n, HALF * h:HALF * h + HALF], diag[0:n, t, tap, 0:n],
                                              CPv[0:n, t, dy + 16 * h:dy + 16 * h + 16, dx:dx + W],
                                              start=(tap == 0), stop=(tap == 8))
                mm.then_inc(b_cp, 1)
            pe.wait_ge(b_da, 1)
            nc.tensor.matmul(ps[3][:, 0:96], c_upper[:], dAT[:, :], start=True, stop=True)
            nc.tensor.matmul(ps[3][:, 128:224], c_ones[:], dAT[:, :], start=True, stop=True)
            pe.wait_ge(b_d1, 1)
            for c in range(NCH):
                mm = nc.tensor.matmul(ps[2][0:NH, Q * c:Q * c + Q], dAT[:, NH * c:NH * c + NH], c_upper[:],
                                      start=True, stop=True)
            mm.then_inc(b_cs, 1)
            pe.wait_ge(b_si, 5)
            pe.wait_ge(b_z, 5)
            pe.wait_ge(b_csc, 6)
            pe.wait_ge(b_dec, 2)
            for c in range(NCH):
                tok = slice(Q * c, Q * c + Q)
                if c >= 1:
                    pe.wait_ge(b_xdt, c)
                    pe.wait_ge(b_bt, c)
                for t in range(ZT):
                    nc.tensor.transpose(ps[3][:, 128 * t:128 * t + 128], XC[:, t, tok], c_ident[:])
                nc.tensor.transpose(ps[3][:, 384:416], Bn[0:32, tok], c_ident[0:32, 0:32]).then_inc(b_tr, 1)
                pe.wait_ge(b_csb, c + 1)
                if c >= 1:
                    pe.wait_ge(b_exc, c)
                for g in range(3):
                    P = (ps[0][:, 0:HALF], ps[0][:, HALF:L], ps[1][:, 0:HALF])[g]
                    nc.tensor.matmul(P, csl[0:44, tok], csb[0:44, c % 2, HALF * g:HALF * g + HALF], start=True, stop=False)
                    mm = nc.tensor.matmul(P, c_identb[:], c_mask[:].unsqueeze(1).to_broadcast([128, 4, Q]),
                                          start=False, stop=True)
                mm.then_inc(b_ex, 1)
                if c >= 1:
                    pe.wait_ge(b_att, c)
                nc.tensor.matmul(ps[1][:, HALF:HALF + Q], Bn[0:32, tok], Cn[0:32, tok], start=True, stop=True).then_inc(b_g, 1)
                if c >= 1:
                    pe.wait_ge(b_yc, c)
                    pe.wait_ge(b_pr, c)
                for t in range(ZT):
                    nc.tensor.matmul(ps[2][:, 128 * t:128 * t + 128], prev[0:32, c % 2, 128 * t:128 * t + 128],
                                     Cn[0:32, tok], start=True, stop=True)
                for t in range(ZT):
                    mm = nc.tensor.matmul(ps[3][:, HALF + 128 * t:HALF + 128 * t + 128],
                                          c_selhead[0:NH, 128 * t:128 * t + 128], csr[0:NH, tok],
                                          start=True, stop=True)
                mm.then_inc(b_y, 1)
                pe.wait_ge(b_att, c + 1)
                pe.wait_ge(b_xdt, c + 1)
                for h in range(NH):
                    r = HP * (h % 4)
                    mm = nc.tensor.matmul(ps[2][r:r + HP, HALF + 128 * (h // 4):HALF + 128 * (h // 4) + 128],
                                          XDT[:, c % 2, HP * h:HP * h + HP], EX[:, c % 2, Q * h:Q * h + Q],
                                          start=True, stop=True)
                mm.then_inc(b_y, 1)
                pe.wait_ge(b_xw, c + 1)
                pe.wait_ge(b_bt, c + 1)
                pe.wait_ge(b_ec, c + 1)
                nc.tensor.matmul(ps[3][0:32, HALF:HALF + DI], BT[:, c % 2, :], XW[:, c % 2, :],
                                 start=True, stop=True).then_inc(b_y, 1)
            for src, ready, done, P in ((Yn, b_yx, b_mu, ps[0]), (SQ, b_sq, b_va, ps[1])):
                pe.wait_ge(ready, ZT)
                for h in range(2):
                    for t in range(ZT):
                        mm = nc.tensor.matmul(P[:, HALF * h:HALF * h + HALF], c_mean[:],
                                              src[:, t, HALF * h:HALF * h + HALF], start=(t == 0), stop=(t == ZT - 1))
                mm.then_inc(done, 1)
            pe.wait_ge(b_gz, ZT)
            for o, n in enumerate(CT):
                for h in range(2):
                    for t in range(ZT):
                        mm = nc.tensor.matmul(ps[2 + o][0:n, HALF * h:HALF * h + HALF], w_o[:, t, 128 * o:128 * o + n],
                                              Yn[:, t, HALF * h:HALF * h + HALF], start=(t == 0), stop=(t == ZT - 1))
                mm.then_inc(b_o, 1)

        def mix_act(act):
            act.wait_ge(b_z, 2)
            for i in range(7):
                n = 128 if i < 6 else 64
                act.wait_ge(b_zp, i + 1)
                if i < 3:
                    nc.scalar.activation(Z[:, i, :], ps[i % 2][:], ACT.Copy).then_inc(b_zc, 1)
                else:
                    nc.scalar.activation(CPv[0:n, i - 3, 1:1 + H, 1:1 + W], ps[i % 2][0:n, :].rearrange(
                        "p (h w) -> p h w", w=W), ACT.Copy).then_inc(b_zc, 1)
            act.wait_ge(b_d2, 1)
            nc.scalar.activation(e_t[:, :], e_t[:, :], ACT.Exp).then_inc(b_d3, 1)
            act.wait_ge(b_d3, 1)
            nc.scalar.activation(e_t[:, :], e_t[:, :], ACT.Ln, bias=1.0).then_inc(b_d3, 1)
            for t in range(3):
                act.wait_ge(b_cp, t + 1)
                nc.scalar.activation(XC[:, t, :], ps[t % 2][:], ACT.Silu, bias=v_mcb[:, t:t + 1]).then_inc(b_si, 1)
            act.wait_ge(b_cp, 4)
            nc.scalar.activation(Bn[0:32, :], ps[1][0:32, :], ACT.Silu, bias=v_mcb[0:32, 3:4]).then_inc(b_si, 1)
            nc.scalar.activation(Cn[0:32, :], ps[1][32:64, :], ACT.Silu, bias=v_mcbC[:]).then_inc(b_si, 1)
            act.wait_ge(b_dif, 1)
            nc.scalar.activation(dte[:, :], dte[:, :], ACT.Exp).then_inc(b_dec, 1)
            nc.scalar.activation(dec[:, :], dec[:, :], ACT.Exp).then_inc(b_dec, 1)
            for c in range(NCH):
                act.wait_ge(b_xdt, c + 1)
                if c >= 2:
                    act.wait_ge(b_y, 3 * (c - 1))
                nc.scalar.activation(BT[:, c % 2, :], ps[3][:, 384:416], ACT.Copy).then_inc(b_bt, 1)
                act.wait_ge(b_ex, c + 1)
                if c >= 2:
                    act.wait_ge(b_y, 3 * (c - 1))
                nc.scalar.activation(EX[:, c % 2, 0:L], ps[0][:], ACT.Exp)
                nc.scalar.activation(EX[:, c % 2, L:L + HALF], ps[1][:, 0:HALF], ACT.Exp).then_inc(b_exc, 1)
                act.wait_ge(b_y, 3 * c + 1)
                if c >= 2:
                    act.wait_ge(b_yc, c - 1)
                nc.scalar.activation(ECS[:, c % 2, :], ps[3][:, HALF:HALF + DI], ACT.Exp).then_inc(b_ec, 1)
            for t in range(ZT):
                act.wait_ge(b_ce, t + 1)
                nc.scalar.activation(SQ[:, t, :], Yn[:, t, :], ACT.Square).then_inc(b_sq, 1)
            act.wait_ge(b_va, 1)
            nc.scalar.activation(csb_all[:, 0:L], ps[1][:], ACT.Sqrt, bias=v_eps5[:], scale=C / DI).then_inc(b_sd, 1)

        csb_all = csb.rearrange("p a b -> p (a b)")

        def mix_dve(dve):
            def heads(v):
                return v.unsqueeze(2).to_broadcast([v.shape[0], NH, HP])

            dve.wait_ge(b_dp, 1)
            bias = v_dtb3[:].unsqueeze(1).to_broadcast([128, NCH, NH])
            e3 = e_t.rearrange("p (c h) -> p c h", h=NH)
            nc.vector.tensor_tensor(dtT[:, :, :], ps[2][:, 0:96].rearrange("p (c h) -> p c h", h=NH), bias,
                                    ALU.add).then_inc(b_d1, 1)
            dve.wait_ge(b_d1, 1)
            nc.vector.tensor_scalar(e3, dtT[:, :, :], SOFTPLUS_LINEAR, None, ALU.min).then_inc(b_d2, 1)
            dve.wait_ge(b_d3, 2)
            nc.vector.tensor_tensor(dtT[:, :, :], dtT[:, :, :], e3, ALU.max).then_inc(b_dt, 1)
            dve.wait_ge(b_dt, 1)
            nc.vector.tensor_tensor(dAT.rearrange("p (c h) -> p c h", h=NH), dtT[:, :, :],
                                    v_na3[:].unsqueeze(1).to_broadcast([128, NCH, NH]), ALU.mult).then_inc(b_da, 1)
            dve.wait_ge(b_cs, 1)
            nc.vector.tensor_copy(csr[0:NH, :], ps[2][0:NH, :]).then_inc(b_csc, 1)
            dve.wait_ge(b_z, 4)
            nc.vector.tensor_scalar(csl[32:32 + NH, :], ps[2][0:NH, :], -1.0, None, ALU.mult).then_inc(b_csc, 1)
            nc.vector.tensor_copy(cst[:, :], ps[3][:, 0:96]).then_inc(b_csc, 1)
            nc.vector.tensor_copy(dec[:, :], ps[3][:, 128:224]).then_inc(b_csc, 1)
            dve.wait_ge(b_csc, 4)
            for q in range(2):
                nc.vector.tensor_copy(csb[32:32 + NH, q, :].rearrange("p (h q) -> p h q", q=Q),
                                      c_heads[32:32 + NH, :].unsqueeze(2).to_broadcast([NH, NH, Q])).then_inc(b_csc, 1)
            nc.vector.tensor_tensor(dte[:, :], dec[:, :], cst[:, :], ALU.subtract).then_inc(b_dif, 1)
            for c in range(NCH):
                tok = slice(Q * c, Q * c + Q)
                dve.wait_ge(b_tr, c + 1)
                if c >= 2:
                    dve.wait_ge(b_y, 3 * (c - 1))
                    dve.wait_ge(b_xw, c - 1)
                nc.vector.tensor_tensor(XDT[:, c % 2, :].rearrange("p (h q) -> p h q", q=HP),
                                        ps[3][:, 0:DI].rearrange("p (h q) -> p h q", q=HP), heads(dtT[:, c, :]),
                                        ALU.mult).then_inc(b_xdt, 1)
                dve.wait_ge(b_exc, c + 1)
                dve.wait_ge(b_g, c + 1)
                att = EX[:, c % 2, :].rearrange("p (h q) -> p h q", q=Q)
                nc.vector.tensor_tensor(att, att, ps[1][:, HALF:HALF + Q].unsqueeze(1).to_broadcast([128, NH, Q]),
                                        ALU.mult).then_inc(b_att, 1)
                dve.wait_ge(b_y, 3 * c + 2)
                dve.wait_ge(b_ec, c + 1)
                nc.vector.tensor_tensor(t1[:, :], ps[2][:, 0:DI], ECS[:, c % 2, :], ALU.mult).then_inc(b_y1, 1)
                dve.wait_ge(b_y1, c + 1)
                nc.vector.tensor_tensor(Yn[:, :, tok], ps[2][:, HALF:HALF + DI].rearrange("p (t q) -> p t q", q=Q),
                                        t1.rearrange("p (t q) -> p t q", q=Q), ALU.add).then_inc(b_yc, 1)
                nc.vector.tensor_tensor(st_t[0:32, :].rearrange("p (h q) -> p h q", q=HP),
                                        prev[0:32, c % 2, :].rearrange("p (h q) -> p h q", q=HP),
                                        heads(dec[0:32, NH * c:NH * c + NH]), ALU.mult).then_inc(b_pd, 1)
                dve.wait_ge(b_pd, c + 1)
                dve.wait_ge(b_y, 3 * c + 3)
                nc.vector.tensor_tensor(prev[0:32, (c + 1) % 2, :], ps[3][0:32, HALF:HALF + DI], st_t[0:32, :],
                                        ALU.add).then_inc(b_pr, 1)
            dve.wait_ge(b_yc, NCH)
            for t in range(ZT):
                nc.vector.scalar_tensor_tensor(Yn[:, t, :], XC[:, t, :], v_d3[:, t:t + 1], Yn[:, t, :], ALU.mult,
                                               ALU.add).then_inc(b_yx, 1)
            dve.wait_ge(b_mu, 1)
            for t in range(ZT):
                nc.vector.scalar_tensor_tensor(Yn[:, t, :], ps[0][:], -C / DI, Yn[:, t, :], ALU.mult,
                                               ALU.add).then_inc(b_ce, 1)
            dve.wait_ge(b_sd, 1)
            nc.vector.reciprocal(csb_all[:, 0:L], csb_all[:, 0:L]).then_inc(b_rs, 1)
            dve.wait_ge(b_rs, 1)
            for t in range(ZT):
                nc.vector.scalar_tensor_tensor(Yn[:, t, :], Yn[:, t, :], v_nw[:, t:t + 1], csb_all[:, 0:L], ALU.mult,
                                               ALU.mult).then_inc(b_n1, 1)
            dve.wait_ge(b_n1, ZT)
            for t in range(ZT):
                nc.vector.scalar_tensor_tensor(Yn[:, t, :], Yn[:, t, :], v_nb[:, t:t + 1], Z[:, t, :], ALU.add,
                                               ALU.mult).then_inc(b_gz, 1)
            for o, n in enumerate(CT):
                dve.wait_ge(b_o, o + 1)
                nc.vector.tensor_tensor(X[0:n, o, :], X[0:n, o, :], ps[2 + o][0:n, :], ALU.add).then_inc(b_x, 1)

        def mix_pool(pool):
            pool.wait_ge(k_x, 2)
            pool.memset(CP[:, :, :], 0.0).then_inc(b_z, 1)
            pool.memset(prev[0:32, 0, :], 0.0).then_inc(b_z, 1)
            pool.memset(csb[0:44, :, :], 0.0).then_inc(b_z, 1)
            pool.memset(csl[0:44, :], 0.0).then_inc(b_z, 1)
            pool.wait_ge(b_z, 4)
            pool.memset(csl[0:NH, :], 1.0).then_inc(b_z, 1)
            pool.wait_ge(b_csc, 4)
            pool.wait_ge(b_dec, 1)
            for c in range(NCH):
                if c >= 2:
                    pool.wait_ge(b_ex, c - 1)
                pool.tensor_tensor(csb[0:NH, c % 2, :].rearrange("p (h q) -> p h q", q=Q),
                                   csr[0:NH, Q * c:Q * c + Q].unsqueeze(1).to_broadcast([NH, NH, Q]),
                                   c_heads[0:NH, :].unsqueeze(2).to_broadcast([NH, NH, Q]),
                                   ALU.mult).then_inc(b_csb, 1)
                pool.wait_ge(b_xdt, c + 1)
                if c >= 2:
                    pool.wait_ge(b_y, 3 * (c - 1))
                pool.tensor_tensor(XW[:, c % 2, :].rearrange("p (h q) -> p h q", q=HP),
                                   XDT[:, c % 2, :].rearrange("p (h q) -> p h q", q=HP),
                                   dte[:, NH * c:NH * c + NH].unsqueeze(2).to_broadcast([128, NH, HP]),
                                   ALU.mult).then_inc(b_xw, 1)

        a_one = sem("attn_ones_set")
        for sm in sems:
            pass
        done = [a_x, m_x, k_x, b_x][phases - 1]

        with nc.Fori(0, n_batch) as b:
            with nc.Block() as block:
                @block.sync
                def _(sp):
                    for c, m in enumerate(CT):
                        sp.dma_start(X[0:m, c, :], x[b, 128 * c:128 * c + m, :]).then_inc(s_x, 16)
                    sp.wait_ge(done, 2)
                    for c, m in enumerate(CT):
                        sp.dma_start(out[b, 128 * c:128 * c + m, :], X[0:m, c, :]).then_inc(s_out, 16)
                    sp.wait_ge(s_out, 32)

                @block.tensor
                def _(pe):
                    norm_pe(pe, 0)
                    pe.wait_ge(a_one, 1)
                    attn_pe(pe)
                    if phases > 1:
                        norm_pe(pe, 1)
                        scan_pe(pe)
                    if phases > 2:
                        norm_pe(pe, 2)
                        conv_pe(pe)
                    if phases > 3:
                        norm_pe(pe, 3)
                        mix_pe(pe)

                @block.scalar
                def _(act):
                    norm_act(act, 0)
                    attn_act(act)
                    if phases > 1:
                        norm_act(act, 1)
                        scan_act(act)
                    if phases > 2:
                        norm_act(act, 2)
                        conv_act(act)
                    if phases > 3:
                        norm_act(act, 3)
                        mix_act(act)

                @block.vector
                def _(dve):
                    dve.wait_ge(s_x, 32)
                    norm_dve(dve, 0, lambda t, n: XN[0:n, t, :])
                    attn_dve(dve)
                    if phases > 1:
                        dve.wait_ge(a_x, 2)
                        norm_dve(dve, 1, lambda t, n: XN[0:n, t, :])
                        scan_dve(dve)
                    if phases > 2:
                        dve.wait_ge(m_x, 2)
                        dve.wait_ge(k_z, 1)
                        norm_dve(dve, 2, lambda t, n: XPv[0:n, t, 1:1 + H, 1:1 + W])
                        conv_dve(dve)
                    if phases > 3:
                        dve.wait_ge(k_x, 2)
                        norm_dve(dve, 3, lambda t, n: XN[0:n, t, :])
                        mix_dve(dve)

                @block.gpsimd
                def _(pool):
                    pool.memset(V[:, :, :, DH:64], 1.0).then_inc(a_one, 1)
                    if phases > 1:
                        scan_pool(pool)
                    if phases > 2:
                        conv_pool(pool)
                    if phases > 3:
                        mix_pool(pool)

            for s in sems:
                nc.sync.sem_clear(s)
            nc.all_engine_barrier()


def layout(inp):
    import numpy as np

    f = {k: np.ascontiguousarray(v) for k, v in inp.items()}
    wqkv = f["L0_conv_qkv_w"].T

    def pairs(w):
        o = np.zeros((C, HEADS, 64), w.dtype)
        o[:, :, :DH] = w.reshape(C, HEADS, DH)
        return o.reshape(C, 64 * HEADS)

    def stacks(xp):
        o = np.zeros((C, K, 2, 102), xp.dtype)
        for s in range(K):
            g, j = s // 2, s % 2
            for order in range(2):
                for part in range(3):
                    at = 32 * part + 16 * order
                    o[:, s, order, at:at + N] = xp[:, 2 * g + order, R + N * j:R + N * j + N]
            o[:, s, j, 96:96 + R] = xp[:, s, :R]
        return o

    xp = f["L1_conv_x_proj_weight"].transpose(2, 0, 1)
    ipw = f["L3_conv_in_proj_w"].T
    d = {
        "x": f["x"].reshape(B, C, L),
        "wq": pairs(wqkv[:, :C]), "wk": pairs(wqkv[:, C:2 * C]), "wv": wqkv[:, 2 * C:],
        "wp": f["L0_conv_proj_w"].T, "pb": f["L0_conv_proj_b"],
        "xpw": stacks(xp),
        "dtw": f["L1_conv_dt_projs_weight"].transpose(2, 0, 1),
        "dtb": f["L1_conv_dt_projs_bias"], "alog": f["L1_conv_A_logs"].reshape(K, C, N),
        "ds": f["L1_conv_Ds"].reshape(K, C), "lnw": f["L1_conv_ln_weight"], "lnb": f["L1_conv_ln_bias"],
        "cw": f["L2_conv_weight"].reshape(C, 9), "cb": f["L2_conv_bias"],
        "wz": ipw[:, :DI], "wx": ipw[:, DI:2 * DI + 2 * NS], "wdt": ipw[:, 2 * DI + 2 * NS:],
        "mcw": f["L3_conv_conv_w"].reshape(DI + 2 * NS, 9), "mcb": f["L3_conv_conv_b"],
        "dtb3": f["L3_conv_dt_bias"], "alog3": f["L3_conv_A_log"], "d3": f["L3_conv_D"],
        "nw": f["L3_conv_norm_w"], "nb": f["L3_conv_norm_b"], "wo": f["L3_conv_out_proj_w"].T,
    }
    return {k: np.ascontiguousarray(v) for k, v in d.items()}


def kernel(**inputs):
    import numpy as np
    import concourse.bacc as bacc
    from concourse.bass_utils import run_bass_kernel_spmd

    nc = bacc.Bacc("TRN2", target_bir_lowering=False, num_devices=1)
    arrays, args = {}, {}
    for name, a in {**layout(inputs), **consts()}.items():
        arrays[f"in_{name}"] = a
        args[name] = nc.dram_tensor(f"in_{name}", a.shape, mybir.dt.from_np(a.dtype), kind="ExternalInput").ap()
    args["out"] = nc.dram_tensor("out_x", (B, C, L), F32, kind="ExternalOutput").ap()
    build(nc, **args)
    r = run_bass_kernel_spmd(nc, [arrays], core_ids=[0])
    return r.results[0]["out_x"].reshape(B, C, H, W)
```

```python
from contextlib import ExitStack

import concourse.bass as bass
from concourse import mybir

F32 = mybir.dt.float32
BF16 = mybir.dt.bfloat16
ALU = mybir.AluOpType
ACT = mybir.ActivationFunctionType
AX = mybir.AxisListType

B, C, H, W = 16, 192, 32, 32
L = H * W
HALF = 512
CT = [128, C - 128]
HEADS, DH = 6, 32
K, N, R = 4, 16, 6
TOP = 30
NH, HP, NS = 12, 32, 32
DI = NH * HP
ZT = DI // 128
Q = 128
NCH = L // Q
STACK = 2 * 32 + 2 * NH
PAD = H + 2
SOFTPLUS_LINEAR = 30.0
REPLACED = -3.0e38


def consts():
    import numpy as np

    ch = np.arange(C)
    same = (ch[:, None] // 6 == ch[None, :] // 6).astype(np.float32) / 6
    group = np.zeros((128, 2, 256), np.float32)
    group[:, 0, :C] = same[:128]
    group[:64, 1, :C] = same[128:]
    row = np.arange(96)[:, None, None] % 32
    blk = np.arange(48)[None, :, None]
    half = np.arange(128)[None, None, :] // 64
    sel_n = np.where(blk < 32, row == blk, row == blk - 32 + 16 * half).astype(np.float32)
    h = np.arange(NH)
    stack = np.zeros((STACK, NH + 2), np.float32)
    sel_head = np.zeros((STACK, DI), np.float32)
    for part in range(3):
        for sign in range(2):
            rows = 32 * part + NH * sign + h
            stack[rows, h] = 1
            stack[rows, NH + sign] = 1
        sel_head[32 * part + h] = h[:, None] == np.arange(DI)[None, :] // HP
    i = np.arange(128)
    return {
        "ident": np.eye(128, dtype=np.float32),
        "group": group,
        "ones": np.ones((128, 128), np.float32),
        "sel_n": sel_n.reshape(96, 48 * 128),
        "upper": (i[:, None] <= i[None, :]).astype(np.float32),
        "head_blocks": stack,
        "sel_head": sel_head,
        "mask": np.where(i[:, None] <= i[None, :], 0, -1e30).astype(np.float32),
    }


def build(nc, x, out, wqk, wv, wp, pb, xpw, dtw, dtb, alog, ds, lnw, lnb, cw, cb, wz, wx, wdt,
          mcw, mcb, dtb3, alog3, d3, nw, nb, wo, ident, group, ones, sel_n, upper, head_blocks,
          sel_head, mask, n_batch=B, phases=4):
    ctx = ExitStack()
    with ctx:
        def sb(name, shape, dt=F32):
            return ctx.enter_context(nc.sbuf_tensor(name, shape, dt))

        sems = []

        def sem(name):
            s = ctx.enter_context(nc.semaphore(name))
            sems.append(s)
            return s

        c_ident = sb("c_ident", [128, 128])
        c_identb = sb("c_identb", [128, 128], BF16)
        c_group = sb("c_group", [128, 2, 256])
        c_ones = sb("c_ones", [128, 128])
        c_mean = sb("c_mean", [128, 128])
        c_sel = sb("c_sel", [128, 48 * 128], BF16)
        c_upper = sb("c_upper", [128, 128])
        c_heads = sb("c_heads", [STACK, NH + 2])
        c_selhead = sb("c_selhead", [STACK, DI], BF16)
        dt_rows = sb("dt_rows", [128, K * C])
        c_mask = sb("c_mask", [128, 128], BF16)
        w_qk = sb("w_qk", [128, 2, 3 * 128])
        w_v = sb("w_v", [128, 2, C])
        w_p = sb("w_p", [128, 2, C])
        v_pb = sb("v_pb", [128, 2])
        w_xp = sb("w_xp", [128, 2, K, 102])
        w_dt = dt_rows[:].rearrange("p (k c) -> p k c", k=K)
        v_dtb = sb("v_dtb", [128, 6])
        v_dtb2 = sb("v_dtb2", [64, K])
        v_na = sb("v_na", [128, 6, N])
        v_ds = sb("v_ds", [128, 6])
        v_lnw = sb("v_lnw", [128, 2])
        v_lnb = sb("v_lnb", [128, 2])
        v_cw = sb("v_cw", [128, 2, 9])
        v_cb = sb("v_cb", [128, 2])
        w_z = sb("w_z", [128, 2, DI])
        w_x = sb("w_x", [128, 2, DI + 2 * NS])
        w_dt3 = sb("w_dt3", [128, 2, NH])
        v_mcw = sb("v_mcw", [128, 4, 9])
        v_mcb = sb("v_mcb", [128, 4])
        v_mcbC = sb("v_mcbC", [32, 1])
        v_dtb3 = sb("v_dtb3", [128, NH])
        v_na3 = sb("v_na3", [128, NH])
        v_d3 = sb("v_d3", [128, ZT])
        v_nw = sb("v_nw", [128, ZT])
        v_nb = sb("v_nb", [128, ZT])
        w_o = sb("w_o", [128, ZT, C])
        diag = sb("diag", [64, 9, 64])
        v_eps5 = sb("v_eps5", [128, 1])
        d_sum = sb("d_sum", [128, 3])
        d_diag = sb("d_diag", [128, 3, 128])

        X = sb("X", [128, 2, L])
        XI = sb("XI", [128, 2, L])
        XN = sb("XN", [128, 2, L])
        g_st = sb("g_st", [128, 2, 2, 6])
        g_mv = sb("g_mv", [128, 2, 3])
        g_t = sb("g_t", [128, 2, 4])

        WORDS = 33600
        arena = sb("arena", [128, WORDS])
        used = [0]

        def area(shape, dt=F32):
            n = 1
            for s in shape:
                n *= s
            words = n if dt == F32 else (n + 1) // 2
            v = arena[:, used[0]:used[0] + words]
            used[0] += words
            assert used[0] <= WORDS, used[0]
            if dt != F32:
                v = v.bitcast(dt)
            if len(shape) > 1:
                names = "abcd"[:len(shape)]
                v = v.rearrange(f"p ({' '.join(names)}) -> p {' '.join(names)}",
                                **{n_: s for n_, s in zip(names[1:], shape[1:])})
            return v

        ps = [ctx.enter_context(nc.psum_tensor(f"ps{i}", [128, L], F32)) for i in range(4)]

        s_ld = sem("weights_loaded")
        s_ld2 = sem("weights_loaded_by_gpsimd")
        s_w = sem("tables_worked_out")
        s_ds = sem("d_sums_ready")
        s_we = sem("exponentials_ready")

        used[0] = 0
        sel_f = area([48 * 128])
        mask_f = area([128])
        selhead_f = area([DI])
        with nc.Block() as block:
            loads = []

            def two(dst, src):
                loads.append((dst[0:128, 0], src[0:128]))
                loads.append((dst[0:64, 1], src[128:192]))

            loads += [(c_ident[:], ident), (c_group[:], group), (c_ones[:], ones), (sel_f[0:96, :], sel_n),
                      (c_upper[:], upper), (c_heads[:], head_blocks), (selhead_f[0:STACK, :], sel_head),
                      (mask_f[:, :], mask)]
            two(w_qk, wqk)
            two(w_v, wv)
            two(w_p, wp)
            two(v_pb, pb)
            two(w_xp, xpw)
            loads.append((w_dt[96:102], dtw))
            for src, dst in ((dtb, v_dtb), (ds, v_ds), (alog, v_na)):
                for t, k in enumerate((0, 2, 1, 3)):
                    loads.append((dst[0:128, t], src[k, 0:128]))
                for t, ks in ((4, (0, 1)), (5, (2, 3))):
                    loads.append((dst[0:64, t], src[ks[0], 128:192]))
                    loads.append((dst[64:128, t], src[ks[1], 128:192]))
            for k in range(K):
                loads.append((v_dtb2[0:64, k], dtb[k, 128:192]))
            two(v_lnw, lnw)
            two(v_lnb, lnb)
            two(v_cw, cw)
            two(v_cb, cb)
            two(w_z, wz)
            two(w_x, wx)
            two(w_dt3, wdt)
            for t in range(4):
                n = min(128, DI + 2 * NS - 128 * t)
                loads.append((v_mcw[0:n, t], mcw[128 * t:128 * t + n]))
                loads.append((v_mcb[0:n, t], mcb[128 * t:128 * t + n]))
            loads.append((v_mcbC[:], mcb[DI + NS:DI + 2 * NS]))
            loads.append((v_dtb3[:], dtb3.partition_broadcast(128)))
            loads.append((v_na3[:], alog3.partition_broadcast(128)))
            for h in range(NH):
                loads.append((v_d3[HP * (h % 4):HP * (h % 4) + HP, h // 4:h // 4 + 1],
                              d3[h:h + 1].partition_broadcast(HP)))
            for t in range(ZT):
                loads.append((v_nw[:, t], nw[128 * t:128 * t + 128]))
                loads.append((v_nb[:, t], nb[128 * t:128 * t + 128]))
                loads.append((w_o[:, t], wo[128 * t:128 * t + 128]))

            hw, hw2, sw = loads[0::3], loads[1::3], loads[2::3]

            def load(queue, part, done):
                for dst, src in part:
                    if len(dst.shape) < len(src.shape):
                        dst = dst.unsqueeze(len(dst.shape))
                    if len(src.shape) < len(dst.shape):
                        src = src.unsqueeze(len(src.shape))
                    queue.dma_start(dst, src).then_inc(done, 16)

            @block.sync
            def _(sp):
                load(sp, hw, s_ld)

            @block.gpsimd
            def _(pool):
                load(pool, sw, s_ld2)

            @block.scalar
            def _(act):
                load(act, hw2, s_ld)
                act.wait_ge(s_ld, 16 * (len(hw) + len(hw2)))
                act.wait_ge(s_ld2, 16 * len(sw))
                nc.scalar.activation(v_na[:], v_na[:], ACT.Exp).then_inc(s_we, 1)
                nc.scalar.activation(v_na3[:], v_na3[:], ACT.Exp).then_inc(s_we, 1)

            @block.vector
            def _(dve):
                dve.wait_ge(s_ld, 16 * (len(hw) + len(hw2)))
                dve.wait_ge(s_ld2, 16 * len(sw))
                nc.vector.tensor_copy(c_identb[:], c_ident[:]).then_inc(s_w, 1)
                nc.vector.tensor_copy(c_sel[0:96], sel_f[0:96, :]).then_inc(s_w, 1)
                nc.vector.tensor_copy(c_mask[:], mask_f[:, :]).then_inc(s_w, 1)
                nc.vector.tensor_copy(c_selhead[:], selhead_f[0:STACK, :]).then_inc(s_w, 1)
                nc.vector.tensor_scalar(c_mean[:], c_ones[:], 1.0 / C, None, ALU.mult).then_inc(s_w, 1)
                nc.vector.memset(v_eps5[:], 1e-5).then_inc(s_w, 1)
                nc.vector.memset(g_mv[:], 0.0).then_inc(s_w, 1)
                for tap in range(9):
                    nc.vector.tensor_scalar(diag[:, tap, :], c_ident[0:64, 0:64], v_mcw[0:64, 3, tap:tap + 1],
                                            None, ALU.mult).then_inc(s_w, 1)
                nc.vector.tensor_tensor(d_sum[:], v_ds[:, 0:6:2], v_ds[:, 1:6:2], ALU.add).then_inc(s_ds, 1)
                dve.wait_ge(s_ds, 1)
                for g in range(3):
                    nc.vector.tensor_scalar(d_diag[:, g, :], c_ident[:], d_sum[:, g:g + 1], None,
                                            ALU.mult).then_inc(s_w, 1)
                dve.wait_ge(s_we, 2)
                nc.vector.tensor_scalar(v_na[:], v_na[:], -1.0, None, ALU.mult).then_inc(s_w, 1)
                nc.vector.tensor_scalar(v_na3[:], v_na3[:], -1.0, None, ALU.mult).then_inc(s_w, 1)

        g_stat = sem("group_stats_ready")
        g_sum = sem("group_sums_ready")
        g_var = sem("group_var_ready")
        g_std = sem("group_std_ready")
        g_dve = sem("group_norm_dve_steps")
        g_xn = sem("normalised_ready")

        def norm_stats(h, x_in=X):
            for t, n in enumerate(CT):
                nc.vector.bn_stats(g_st[0:n, t, h, :], x_in[0:n, t, HALF * h:HALF * h + HALF]).then_inc(g_dve, 1)

        def norm_dve(dve, u, writes, x_in=X, begun=False, room=None):
            if not begun:
                norm_stats(0, x_in)
            norm_stats(1, x_in)
            for t, n in enumerate(CT):
                dve.wait_ge(g_dve, 9 * u + 4)
                nc.vector.bn_aggr(g_mv[0:n, t, 0:2], g_st[0:n, t, :, :]).then_inc(g_dve, 1)
            dve.wait_ge(g_dve, 9 * u + 6)
            nc.vector.tensor_tensor(g_mv[:, :, 2], g_mv[:, :, 0], g_mv[:, :, 0], ALU.mult).then_inc(g_stat, 1)
            dve.wait_ge(g_sum, u + 1)
            both = ps[0][:, 0:16].rearrange("p (t s) -> p t s", s=8)
            nc.vector.tensor_copy(g_t[:, :, 0:3], both[:, :, 0:3]).then_inc(g_dve, 1)
            dve.wait_ge(g_dve, 9 * u + 7)
            nc.vector.tensor_tensor(g_t[:, :, 1], g_t[:, :, 1], g_t[:, :, 2], ALU.add).then_inc(g_dve, 1)
            nc.vector.tensor_tensor(g_t[:, :, 3], g_t[:, :, 0], g_t[:, :, 0], ALU.mult).then_inc(g_dve, 1)
            dve.wait_ge(g_dve, 9 * u + 9)
            nc.vector.tensor_tensor(g_t[:, :, 2], g_t[:, :, 1], g_t[:, :, 3], ALU.subtract).then_inc(g_var, 1)
            dve.wait_ge(g_std, u + 1)
            nc.vector.reciprocal(g_t[:, :, 2], g_t[:, :, 3]).then_inc(g_var, 1)
            dve.wait_ge(g_var, 2 * u + 2)
            if room is not None:
                dve.wait_ge(room, 1)
            for m in range(2):
                for t, n in enumerate(CT):
                    src, dst = (v.rearrange("p (h w) -> p h w", w=W) if len(v.shape) == 2 else v
                                for v in (x_in[0:n, t, :], writes(t, n)))
                    rows = slice(H // 2 * m, H // 2 * (m + 1))
                    nc.vector.tensor_scalar(dst[:, rows, :], src[:, rows, :], g_t[0:n, t, 0:1], g_t[0:n, t, 2:3],
                                            ALU.subtract, ALU.mult).then_inc(g_xn, 1)

        def norm_pe(pe, u):
            pe.wait_ge(g_stat, u + 1)
            for t in range(2):
                for s, m in enumerate(CT):
                    mm = nc.tensor.matmul(ps[0][:, 8 * t:8 * t + 3], c_group[0:m, s, 128 * t:128 * t + 128],
                                          g_mv[0:m, s, :], start=(s == 0), stop=(s == 1))
            mm.then_inc(g_sum, 1)

        def norm_act(act, u):
            act.wait_ge(g_var, 2 * u + 1)
            nc.scalar.activation(g_t[:, :, 3], g_t[:, :, 2], ACT.Sqrt, bias=v_eps5[:, :]).then_inc(g_std, 1)

        s_x = ctx.enter_context(nc.semaphore("image_loaded"))
        s_out = ctx.enter_context(nc.semaphore("image_stored"))

        used[0] = 0
        HI = area([3, L], BF16)
        MI = area([3, L], BF16)
        LO = area([3, L], BF16)
        RS = area([3, L])
        QM = area([HEADS, L], BF16)
        KM = area([HEADS, L], BF16)
        QL = area([HEADS, L], BF16)
        KL = area([HEADS, L], BF16)
        MAIN, REST = 4 * DH, 2 * DH + 1
        V = area([NCH, HEADS, 64])
        MX = area([HEADS * NCH], BF16)
        PT = area([4, L])
        OC = area([L])
        RD = area([L])
        OA = area([2, L])
        PAIRS = HEADS // 2

        a_qk = sem("attn_qk_psum_ready")
        a_qkc = sem("attn_qk_copied")
        a_v = sem("attn_v_psum_ready")
        a_vc = sem("attn_v_copied")
        a_s = sem("attn_rough_scores_ready")
        a_m = sem("attn_row_max_ready")
        a_r = sem("attn_max_rows_ready")
        a_rc = sem("attn_max_rows_copied")
        a_rs = sem("attn_rests_ready")
        a_mi = sem("attn_middle_parts_ready")
        a_lo = sem("attn_low_parts_ready")
        a_dm = [sem(f"attn_operands_ready_{t}") for t in range(HEADS // 2)]
        a_one = sem("attn_ones_set")
        a_st = sem("attn_scores_ready")
        a_e = sem("attn_exp_ready")
        a_pv = sem("attn_exp_used")
        a_rd = sem("attn_denominators_inverted")
        a_o = sem("attn_heads_ready")
        a_oc = sem("attn_sums_copied")
        a_p = sem("attn_projection_ready")
        a_x = sem("attn_added")

        def head_rows(h):
            return h // 2, 64 * (h % 2)

        def place(h, k):
            return (k, DH * h) if h < 4 else (2, 64 * k + DH * (h - 4))

        PARTS = [(("QM", 0, "HI"), ("QM", 1, "HI"), ("QL", 0, "HI"), ("QM", 2, "MI"), ("QM", 3, "MI"), ("QL", 1, "LO")),
                 (("KM", 0, "HI"), ("KM", 2, "HI"), ("KL", 1, "HI"), ("KM", 1, "MI"), ("KM", 3, "MI"), ("KL", 0, "LO"))]
        COPIES = 2 * sum(len(p) for p in PARTS)

        def attn_sp(sp):
            where = {"QM": QM, "QL": QL, "KM": KM, "KL": KL, "HI": HI, "MI": MI, "LO": LO}
            for t in range(PAIRS):
                for part, ready in (("HI", a_qkc), ("MI", a_mi), ("LO", a_lo)):
                    for k in range(2):
                        for h in (2 * t, 2 * t + 1):
                            i, r = place(h, k)
                            sp.wait_ge(ready, i + 1)
                            for dst, at, src in PARTS[k]:
                                if src == part:
                                    sp.dma_start(where[dst][DH * at:DH * at + DH, h, :],
                                                 where[src][r:r + DH, i, :]).then_inc(a_dm[t], 16)

        def attn_pool(pool):
            pool.memset(KL[2 * DH:REST, :, :], 1.0).then_inc(a_one, 1)
            pool.wait_ge(a_one, 1)
            pool.memset(V[:, :, :, DH:64], 1.0).then_inc(a_one, 1)
            for i in range(3):
                pool.wait_ge(a_mi, i + 1)
                pool.tensor_tensor(LO[:, i, :], RS[:, i, :], MI[:, i, :], ALU.subtract).then_inc(a_lo, 1)

        def attn_pe(pe):
            def project(i, P):
                for h in range(2):
                    pe.wait_ge(g_xn, 2 * (h + 1))
                    for c, m in enumerate(CT):
                        mm = nc.tensor.matmul(P[:, HALF * h:HALF * h + HALF], w_qk[0:m, c, 128 * i:128 * i + 128],
                                              XN[0:m, c, HALF * h:HALF * h + HALF], start=(c == 0), stop=(c == 1))
                mm.then_inc(a_qk, 1)

            def values(j):
                if j % 4 == 0:
                    pe.wait_ge(a_rs, j // 4 + 1)
                for c, m in enumerate(CT):
                    mm = nc.tensor.matmul(ps[j // 4][:, 256 * (j % 4):256 * (j % 4) + C],
                                          XN[0:m, c, Q * j:Q * j + Q], w_v[0:m, c, :], start=(c == 0), stop=(c == 1))
                if j % 4 == 3:
                    mm.then_inc(a_v, 1)

            def rough(i, P):
                h, j = i // NCH, i % NCH
                if h < 4:
                    q, k = (HI[DH * h:DH * h + DH, n, :] for n in range(2))
                else:
                    q, k = QM[0:DH, h, :], KM[0:DH, h, :]
                for m in range(2):
                    mm = nc.tensor.matmul(P[:, HALF * m:HALF * m + HALF], q[:, Q * j:Q * j + Q],
                                          k[:, HALF * m:HALF * m + HALF], start=True, stop=True)
                mm.then_inc(a_s, 1)

            def max_rows(t):
                pe.wait_ge(a_m, 2 * NCH * (t + 1))
                for h in (2 * t, 2 * t + 1):
                    r = head_rows(h)[1] + 32
                    for j in range(NCH):
                        mm = nc.tensor.matmul(ps[3][r:r + 1, Q * j:Q * j + Q], MX[:, NCH * h + j:NCH * h + j + 1],
                                              c_identb[:], start=True, stop=True)
                mm.then_inc(a_r, 1)

            project(0, ps[0])
            project(1, ps[1])
            for i in range(2 * NCH):
                if i == 0:
                    pe.wait_ge(a_qkc, 2)
                if i >= 2:
                    pe.wait_ge(a_m, i - 1)
                rough(i, ps[2 + i % 2])
                if 2 <= i < 2 + NCH:
                    values(i - 2)
            max_rows(0)
            project(2, ps[2])
            pe.wait_ge(a_vc, 2)
            for t in range(PAIRS):
                step = 2 * NCH * (t + 1)

                def next_rough():
                    nonlocal step
                    if step < min(2 * NCH * (t + 2), HEADS * NCH):
                        pe.wait_ge(a_m, step)
                        rough(step, ps[3])
                        step += 1

                pe.wait_ge(a_rc, 2 * (t + 1))
                pe.wait_ge(a_dm[t], 16 * COPIES)
                if t == 1:
                    pe.wait_ge(a_dm[2], 16 * COPIES)
                for j in range(NCH + 1):
                    if j < NCH:
                        for m in range(2):
                            for e in range(2):
                                if m == 0 and t + j > 0:
                                    pe.wait_ge(a_e, 2 * (NCH * t + j) - 1 + e)
                                P = ps[e][:, HALF * m:HALF * m + HALF]
                                for q, k, n in ((QM, KM, MAIN), (QL, KL, REST)):
                                    mm = nc.tensor.matmul(P, k[0:n, 2 * t + e, Q * j:Q * j + Q],
                                                          q[0:n, 2 * t + e, HALF * m:HALF * m + HALF],
                                                          start=(n == MAIN), stop=(n == REST))
                                if m == 1:
                                    mm.then_inc(a_st, 1)
                            if m == 1 or j == 2:
                                next_rough()
                    elif t + 1 < PAIRS:
                        max_rows(t + 1)
                    if j >= 1:
                        pe.wait_ge(a_e, 2 * (NCH * t + j))
                        if j == 1:
                            pe.wait_ge(*((a_oc, t) if t > 0 else (a_rs, 3)))
                        for m in range(2):
                            for e in range(2):
                                mm = nc.tensor.matmul(ps[2][64 * e:64 * e + 64, HALF * m:HALF * m + HALF],
                                                      V[:, j - 1, 2 * t + e, :],
                                                      PT[:, 2 * ((j - 1) % 2) + e, HALF * m:HALF * m + HALF],
                                                      start=(j == 1), stop=(j == NCH))
                        mm.then_inc(a_pv, 1)
                        next_rough()
            for c, kk in enumerate(CT):
                for m in range(2):
                    pe.wait_ge(a_o, 4 * (PAIRS - 1) + (2 * m + 2 if c == 1 else 0))
                    for o, n in enumerate(CT):
                        mm = nc.tensor.matmul(ps[o][0:n, HALF * m:HALF * m + HALF], w_p[0:kk, c, 128 * o:128 * o + n],
                                              OA[0:kk, c, HALF * m:HALF * m + HALF], start=(c == 0), stop=(c == 1))
                        if c == 1:
                            mm.then_inc(a_p, 1)

        def attn_act(act):
            def high(i):
                act.wait_ge(a_qk, i + 1)
                nc.scalar.activation(HI[:, i, :], ps[i][:], ACT.Copy).then_inc(a_qkc, 1)

            def middle(i):
                act.wait_ge(a_rs, i + 1)
                nc.scalar.activation(MI[:, i, :], RS[:, i, :], ACT.Copy).then_inc(a_mi, 1)

            high(0)
            high(1)
            middle(0)
            middle(1)
            for g in range(2):
                act.wait_ge(a_v, g + 1)
                nc.scalar.activation(V[:, 4 * g:4 * g + 4, :, 0:DH],
                                     ps[g][:].rearrange("p (j c) -> p j c", j=4)[:, :, 0:C].rearrange(
                                         "p j (h d) -> p j h d", d=DH), ACT.Copy).then_inc(a_vc, 1)

            def guard(t):
                act.wait_ge(a_r, t + 1)
                for e in range(2):
                    nc.scalar.activation(QL[2 * DH:REST, 2 * t + e, :], ps[3][64 * e + 32:64 * e + 33, :], ACT.Copy,
                                         scale=-1.0).then_inc(a_rc, 1)

            guard(0)
            for t in range(PAIRS):
                for j in range(NCH):
                    if NCH * t + j >= 2:
                        act.wait_ge(a_pv, NCH * t + j - 1)
                    for e in range(2):
                        act.wait_ge(a_st, 2 * (NCH * t + j) + e + 1)
                        nc.scalar.activation(PT[:, 2 * (j % 2) + e, :], ps[e][:], ACT.Exp, scale=DH ** -0.5).then_inc(a_e, 1)
                    if t == 0 and j < 2:
                        (high, middle)[j](2)
                if t + 1 < PAIRS:
                    guard(t + 1)
                act.wait_ge(a_pv, NCH * (t + 1))
                if t > 0:
                    act.wait_ge(a_o, 4 * t)
                nc.scalar.activation(OC[:, :], ps[2][:], ACT.Copy).then_inc(a_oc, 1)

        def attn_dve(dve, b):
            def rest(i):
                dve.wait_ge(a_qkc, i + 1)
                nc.vector.tensor_tensor(RS[:, i, :], ps[i][:], HI[:, i, :], ALU.subtract).then_inc(a_rs, 1)

            def maxima(t, both):
                for i in range(2 * NCH * t, 2 * NCH * (t + 1)):
                    dve.wait_ge(a_s, i + 1)
                    P = ps[2 + i % 2] if both else ps[3]
                    nc.vector.reduce_max(MX[:, i:i + 1], P[:], AX.X).then_inc(a_m, 1)
                    if i == 2 * NCH:
                        rest(2)
                    if t == 2:
                        k = i - 2 * NCH * t
                        if k == 0:
                            dve.wait_ge(a_oc, 1)
                        if k < 4:
                            invert(slice(HALF // 2 * k, HALF // 2 * (k + 1)))
                        if k in (2, 4):
                            dve.wait_ge(a_rd, k)
                            scale(0, k // 2 - 1)
            rest(0)
            rest(1)
            maxima(0, True)
            maxima(1, False)
            maxima(2, False)
            divide(dve, 1)
            divide(dve, 2)
            dve.wait_ge(s_out, 32 * b + 1)
            for m in range(2):
                for o, n in enumerate(CT):
                    cols = slice(HALF * m, HALF * m + HALF)
                    dve.wait_ge(a_p, 2 * m + o + 1)
                    nc.vector.scalar_tensor_tensor(X[0:n, o, cols], ps[o][0:n, cols], v_pb[0:n, o:o + 1],
                                                   XI[0:n, o, cols], ALU.add, ALU.add).then_inc(a_x, 1)
                if m == 0:
                    dve.wait_ge(a_x, 2)
                    norm_stats(0)

        def invert(cols):
            nc.vector.reciprocal(RD[:, cols], OC[:, cols]).then_inc(a_rd, 1)

        def scale(t, m):
            cols = slice(HALF * m, HALF * m + HALF)
            for e in range(2):
                h, r = 2 * t + e, 64 * e
                nc.vector.tensor_tensor(OA[DH * (h % 4):DH * (h % 4) + DH, h // 4, cols], OC[r:r + 32, cols],
                                        RD[r + 32:r + 64, cols], ALU.mult).then_inc(a_o, 1)

        def divide(dve, t):
            dve.wait_ge(a_oc, t + 1)
            for m in range(2):
                invert(slice(HALF * m, HALF * m + HALF))
                dve.wait_ge(a_rd, 4 + 2 * (t - 1) + m + 1)
                scale(t, m)

        used[0] = 0
        XT = area([2, L])
        UM = XN[:, 1, :]
        DT = area([6, L])
        DU = area([6, L])
        BC = area([2 * K, L], BF16)
        RES = area([2, L])
        DRK = RES
        dA = area([2, L])
        MID = dA[:, 0, 0:L // 2].bitcast(BF16)
        at_sp = used[0]
        bu = area([2, L])
        hs = area([2, L])
        Cs = area([2, L])
        hc = area([2, L])
        YA = area([2, L])
        SP = arena[:, at_sp:at_sp + 6 * L].rearrange("p (t l) -> p t l", t=6)
        YS = RES[:, 1, :]
        assert used[0] < WORDS
        GROUPS = [(0, 1), (2, 3), (4, 5)]
        DIRS = (0, 2, 1, 3)
        READY = (0, 1, 2, 4, 3, 5)
        COMPLETE = (1, 2, 3, 4, 3, 4)
        MIXED = 3 * 2 * 4

        m_t = sem("scan_inputs_ready")
        m_xd = sem("scan_xdbl_ready")
        m_hi = sem("scan_high_parts_ready")
        m_r = sem("scan_rests_ready")
        m_mid = sem("scan_middle_parts_ready")
        m_bc = sem("scan_bc_ready")
        m_dd = sem("scan_dt_u_ready_two_tiles")
        m_v0 = sem("scan_dt_biased")
        m_v1 = sem("scan_dt_biased_high_channels")
        m_dr = sem("scan_low_rank_dt_copied")
        m_mx = sem("scan_mixed_stacks_ready")
        m_dtp = sem("scan_dt_psum_ready")
        m_cl = sem("scan_dt_clamped")
        m_e = sem("scan_dt_exp")
        m_ln = sem("scan_dt_log")
        m_dt = sem("scan_dt_ready")
        m_du = sem("scan_dtu_ready")
        m_b = [sem(f"scan_b_rows_{g}") for g in range(3)]
        m_c = [sem(f"scan_c_rows_{g}") for g in range(3)]
        m_cc = [sem(f"scan_c_copied_{g}") for g in range(3)]
        m_da = [sem(f"scan_decay_{g}") for g in range(3)]
        m_bu = [sem(f"scan_input_{g}") for g in range(3)]
        m_h = [sem(f"scan_state_{g}") for g in range(3)]
        m_hc = [sem(f"scan_product_{g}") for g in range(3)]
        m_y = [sem(f"scan_product_summed_{g}") for g in range(3)]
        m_yc = sem("scan_group_copied")
        m_ys = sem("scan_y_ready")
        m_mu = sem("scan_mean_ready")
        m_ce = sem("scan_centred")
        m_sq = sem("scan_squares_ready")
        m_va = sem("scan_var_ready")
        m_sd = sem("scan_std_ready")
        m_rs = sem("scan_rstd_ready")
        m_n = sem("scan_normalised")
        m_ge = sem("scan_gelu_ready")
        m_x = sem("scan_added")

        def source(t):
            return (XN[:, 0, :], XN[:, 0, :], XT[:, 0, :], XT[:, 0, :], UM, UM)[t]

        def used_by(sem_, g, e, n):
            if isinstance(n, int) and n == 0 and g > 0:
                return sem_[g - 1], 2 * N + (e + 1)
            return sem_[g], 2 * n + (e + 1)

        def scan_pe(pe):
            for k in range(K + 1):
                if k < K:
                    P = ps[k % 2]
                    if k >= 2:
                        pe.wait_ge(m_r, k - 1)
                        pe.wait_ge(m_t, 2)
                        pe.wait_ge(m_dr, k - 1)
                    for h in range(2):
                        pe.wait_ge(g_xn, 4 + 2 * (h + 1))
                        for c, m in enumerate(CT):
                            mm = nc.tensor.matmul(P[0:102, HALF * h:HALF * h + HALF], w_xp[0:m, c, k, :],
                                                  (XN, XT)[k // 2][0:m, c, HALF * h:HALF * h + HALF],
                                                  start=(c == 0), stop=(c == 1))
                    mm.then_inc(m_xd, 1)
                if k >= 1:
                    pe.wait_ge(m_dr, k)
                    if k >= 2:
                        pe.wait_ge(m_v0, k - 1)
                        pe.wait_ge(m_v1, k - 1)
                    for h in range(2):
                        for c, m in enumerate(CT):
                            mm = nc.tensor.matmul(ps[2 + c][0:m, HALF * h:HALF * h + HALF],
                                                  w_dt[96:102, DIRS[k - 1], 128 * c:128 * c + m],
                                                  DRK[96:102, (k - 1) % 2, HALF * h:HALF * h + HALF],
                                                  start=True, stop=True)
                    mm.then_inc(m_dtp, 1)
            pe.wait_ge(m_bc, K)
            pe.wait_ge(m_v0, K)
            pe.wait_ge(m_v1, K)
            pe.wait_ge(m_t, 3)
            def rows(g, t, e, n):
                for j, P in enumerate((ps[e], ps[2])):
                    if j == 0:
                        pe.wait_ge(*used_by(m_bu, g, e, n))
                    elif e == 0:
                        pe.wait_ge(*used_by(m_cc, g, e, n))
                    else:
                        pe.wait_ge(m_cc[g], 2 * n + (e + 1))
                    at = n * 128 + 128 * (16 * (t % 2) if t < 4 else 32)
                    at = slice(at, at + 128) if isinstance(n, int) else bass.ds(at, 128)
                    stack = (2 * (t // 2) if t < 4 else 4 + 2 * (t - 4)) + j
                    for h in range(2):
                        mm = nc.tensor.matmul(P[:, HALF * h:HALF * h + HALF], c_sel[0:96, at],
                                              BC[0:96, stack, HALF * h:HALF * h + HALF],
                                              start=True, stop=True)
                    mm.then_inc((m_b, m_c)[j][g], 1)

            def add(g, e, n, stop=False):
                pe.wait_ge(m_hc[g], 2 * n + (e + 3))
                for h in range(2):
                    mm = nc.tensor.matmul(ps[3][:, HALF * h:HALF * h + HALF], c_ident[:],
                                          hc[:, e, HALF * h:HALF * h + HALF], start=False, stop=stop,
                                          skip_group_check=True)
                mm.then_inc(m_y[g], 1)

            def first(g):
                if g > 0:
                    pe.wait_ge(m_y[g - 1], 2 * N + 2)
                pe.sem_inc(m_y[g], 2)
                if g > 0:
                    pe.wait_ge(m_yc, g)
                for h in range(2):
                    nc.tensor.matmul(ps[3][:, HALF * h:HALF * h + HALF], d_diag[:, g, :],
                                     source(GROUPS[g][0])[:, HALF * h:HALF * h + HALF], start=True, stop=False,
                                     skip_group_check=True)

            def last(g):
                for e in range(2):
                    add(g, e, N - 1, stop=(e == 1))

            for g, tiles in enumerate(GROUPS):
                if g == 2:
                    pe.wait_ge(m_mx, 16 * MIXED)
                for e, t in enumerate(tiles):
                    rows(g, t, e, 0)
                if g > 0:
                    last(g - 1)
                rows(g, tiles[0], 0, 1)
                first(g)
                add(g, 0, 0)
                rows(g, tiles[1], 1, 1)
                add(g, 1, 0)
                with pe.Fori(2, N) as n:
                    for e, t in enumerate(tiles):
                        rows(g, t, e, n)
                        add(g, e, n - 1)
            last(2)
            for src, ready, each, done, P in ((YA, m_ys, 0, m_mu, ps[0]), (hs, m_sq, 2, m_va, ps[1])):
                for h in range(2):
                    pe.wait_ge(ready, 2 + each * h)
                    for c, m in enumerate(CT):
                        mm = nc.tensor.matmul(P[:, HALF * h:HALF * h + HALF], c_mean[0:m, :],
                                              src[0:m, c, HALF * h:HALF * h + HALF], start=(c == 0), stop=(c == 1))
                    mm.then_inc(done, 1)

        def scan_sp(sp):
            for s in range(K):
                for i in range(2):
                    k = 2 * (s // 2) + i
                    src = 2 * (k % 2) + s % 2
                    sp.wait_ge(m_bc, src + 1)
                    for part in range(3):
                        at, to = 32 * part + 16 * (k // 2), 32 * part + 16 * i
                        sp.dma_start(BC[to:to + N, K + s, :], BC[at:at + N, src, :]).then_inc(m_mx, 16)

        def scan_act(act):
            for c, m in enumerate(CT):
                act.wait_ge(g_xn, 7 + c)
                nc.scalar.activation(XT[0:m, c, :].rearrange("p (w h) -> p w h", h=H),
                                     XN[0:m, c, :].rearrange("p (h w) -> p w h", w=W), ACT.Copy).then_inc(m_t, 1)
            act.wait_ge(m_t, 2)
            nc.scalar.activation(UM[64:128, :], XT[0:64, 1, :], ACT.Copy).then_inc(m_t, 1)
            for k in range(K + 1):
                if k < K:
                    act.wait_ge(m_xd, k + 1)
                    nc.scalar.activation(BC[0:96, k, :], ps[k % 2][0:96, :], ACT.Copy).then_inc(m_hi, 1)
                if k >= 1:
                    t, rows = dt_place(DIRS[k - 1], 1)
                    act.wait_ge(m_dtp, k)
                    nc.scalar.activation(DT[rows, t, :], ps[3][0:64, :], ACT.Identity,
                                         bias=v_dtb2[0:64, DIRS[k - 1]:DIRS[k - 1] + 1]).then_inc(m_v1, 1)
                if k < K:
                    act.wait_ge(m_r, k + 1)
                    nc.scalar.activation(BC[32:64, k, :], RES[32:64, k % 2, :], ACT.Copy).then_inc(m_mid, 1)
                    if k >= 1:
                        act.wait_ge(m_bc, k)
                    nc.scalar.activation(MID[64:96, :], RES[64:96, k % 2, :], ACT.Copy).then_inc(m_mid, 1)
                for i in ((), (), (0,), (1,), (2, 3, 4, 5))[k]:
                    t = READY[i]
                    act.wait_ge(m_cl, i + 1)
                    nc.scalar.activation(SP[:, t, :], SP[:, t, :], ACT.Exp).then_inc(m_e, 1)
            for i, t in enumerate(READY):
                act.wait_ge(m_e, i + 1)
                nc.scalar.activation(SP[:, t, :], SP[:, t, :], ACT.Ln, bias=1.0).then_inc(m_ln, 1)
            act.wait_ge(m_bc, K)
            act.wait_ge(m_dt, 2)

            def step(g, e, n):
                t = GROUPS[g][e]
                act.wait_ge(*used_by(m_h, g, e, n))
                scale = v_na[:, t, n:n + 1] if isinstance(n, int) else v_na[:, t, bass.ds(n, 1)]
                nc.scalar.activation(dA[:, e, :], DT[:, t, :], ACT.Exp, scale=scale).then_inc(m_da[g], 1)
                act.wait_ge(m_c[g], 2 * n + (e + 1))
                if g == 0 and isinstance(n, int):
                    act.wait_ge(m_dt, 6)
                act.wait_ge(*used_by(m_hc, g, e, n))
                nc.scalar.activation(Cs[:, e, :], ps[2][:], ACT.Copy).then_inc(m_cc[g], 1)

            def copy_y(g):
                act.wait_ge(m_y[g], 2 * N + 2)
                for dst, rows in (((YA[:, 0, :], slice(0, 128)),), ((YS[:, :], slice(0, 128)),),
                                  ((YA[0:64, 1, :], slice(0, 64)), (RES[0:64, 0, :], slice(64, 128))))[g]:
                    nc.scalar.activation(dst, ps[3][rows, :], ACT.Copy).then_inc(m_yc, 1)

            for g in range(3):
                act.sem_inc(m_cc[g], 1)
                for e in range(2):
                    step(g, e, 0)
                if g > 0:
                    copy_y(g - 1)
                with act.Fori(1, N) as n:
                    for e in range(2):
                        step(g, e, n)
            copy_y(2)
            halves = [slice(HALF * h, HALF * h + HALF) for h in range(2)]
            for h in range(2):
                for c, m in enumerate(CT):
                    act.wait_ge(m_ce, 2 * h + c + 1)
                    nc.scalar.activation(hs[0:m, c, halves[h]], YA[0:m, c, halves[h]], ACT.Square).then_inc(m_sq, 1)
            for h in range(2):
                act.wait_ge(m_va, h + 1)
                nc.scalar.activation(RES[:, 1, halves[h]], ps[1][:, halves[h]], ACT.Ln, bias=v_eps5[:]).then_inc(m_sd, 1)
            for h in range(2):
                act.wait_ge(m_sd, h + 1)
                nc.scalar.activation(RES[:, 1, halves[h]], RES[:, 1, halves[h]], ACT.Exp, scale=-0.5).then_inc(m_rs, 1)
            for h in range(2):
                for c, m in enumerate(CT):
                    act.wait_ge(m_n, 2 * h + c + 1)
                    nc.scalar.activation(YA[0:m, c, halves[h]], YA[0:m, c, halves[h]], ACT.Gelu, bias=v_lnb[0:m, c:c + 1],
                                         scale=v_lnw[0:m, c:c + 1]).then_inc(m_ge, 1)

        def dt_place(k, c):
            if c == 0:
                return (0, 2, 1, 3)[k], slice(0, 128)
            return 4 + k // 2, slice(64 * (k % 2), 64 * (k % 2) + 64)

        def scan_dve(dve):
            for k in range(K + 1):
                if k < K:
                    dve.wait_ge(m_xd, k + 1)
                    if k >= 2:
                        dve.wait_ge(m_dtp, k - 1)
                    nc.vector.tensor_copy(DRK[96:102, k % 2, :], ps[k % 2][96:102, :]).then_inc(m_dr, 1)
                    dve.wait_ge(m_hi, k + 1)
                    if k >= 2:
                        dve.wait_ge(m_mid, 2 * k - 2)
                    nc.vector.tensor_tensor(RES[0:96, k % 2, :], ps[k % 2][0:96, :], BC[0:96, k, :],
                                            ALU.subtract).then_inc(m_r, 1)
                if k >= 1:
                    t, _ = dt_place(DIRS[k - 1], 0)
                    dve.wait_ge(m_dtp, k)
                    nc.vector.tensor_scalar(DT[:, t, :], ps[2][:], v_dtb[:, t:t + 1], None, ALU.add).then_inc(m_v0, 1)
                if k < K:
                    dve.wait_ge(m_r, k + 1)
                    dve.wait_ge(m_mid, 2 * (k + 1))
                    nc.vector.tensor_tensor(BC[64:96, k, :], RES[64:96, k % 2, :], MID[64:96, :],
                                            ALU.subtract).then_inc(m_bc, 1)
                for i in ((), (0,), (1,), (2, 3), (4, 5))[k]:
                    t = READY[i]
                    dve.wait_ge(m_v0, COMPLETE[t])
                    if t >= 4:
                        dve.wait_ge(m_v1, COMPLETE[t])
                    nc.vector.tensor_scalar(SP[:, t, :], DT[:, t, :], SOFTPLUS_LINEAR, None, ALU.min).then_inc(m_cl, 1)
            dve.sem_inc(m_h[0], 2)
            for i, t in enumerate(READY):
                dve.wait_ge(m_ln, i + 1)
                nc.vector.tensor_tensor(DT[:, t, :], DT[:, t, :], SP[:, t, :], ALU.max).then_inc(m_dt, 1)

            def step(g, e, n):
                t = GROUPS[g][e]
                dve.wait_ge(m_b[g], 2 * n + (e + 1))
                dve.wait_ge(*used_by(m_h, g, e, n))
                nc.vector.tensor_tensor(bu[:, e, :], DU[:, t, :], ps[e][:], ALU.mult).then_inc(m_bu[g], 1)
                dve.wait_ge(m_bu[g], 2 * n + (e + 3))
                dve.wait_ge(m_da[g], 2 * n + (e + 1))
                dve.wait_ge(*used_by(m_hc, g, e, n))
                o = slice(None, None, -1) if e == 1 else slice(None)
                nc.vector.tensor_tensor_scan(hs[:, e, o], dA[:, e, o], bu[:, e, o], 0.0, ALU.mult,
                                             ALU.add).then_inc(m_h[g], 1)

            for g in range(3):
                if g == 0:
                    dve.wait_ge(m_dt, 6)
                for t in ((), (3,), (4, 5))[g]:
                    nc.vector.tensor_tensor(DU[:, t, :], DT[:, t, :], source(t), ALU.mult).then_inc(m_dd, 1)
                if g > 0:
                    dve.wait_ge(m_dd, (1, 3)[g - 1])
                dve.wait_ge(m_du, (2, 3, 3)[g])
                dve.sem_inc(m_bu[g], 2)
                if g > 0:
                    dve.sem_inc(m_h[g], 2)
                for e in range(2):
                    step(g, e, 0)
                with dve.Fori(1, N) as n:
                    for e in range(2):
                        step(g, e, n)
            dve.wait_ge(m_yc, 4)
            nc.vector.tensor_tensor(YA[0:64, 1, :].rearrange("p (h w) -> p h w", w=W), YA[0:64, 1, :].rearrange(
                "p (h w) -> p h w", w=W), RES[0:64, 0, :].rearrange("p (w h) -> p h w", h=H), ALU.add).then_inc(m_ys, 1)
            halves = [slice(HALF * h, HALF * h + HALF) for h in range(2)]
            for h in range(2):
                dve.wait_ge(m_mu, h + 1)
                for c, m in enumerate(CT):
                    nc.vector.tensor_tensor(YA[0:m, c, halves[h]], YA[0:m, c, halves[h]], ps[0][0:m, halves[h]],
                                            ALU.subtract).then_inc(m_ce, 1)
            for h in range(2):
                dve.wait_ge(m_rs, h + 1)
                for c, m in enumerate(CT):
                    dve.wait_ge(m_sq, 2 * h + c + 1)
                    nc.vector.tensor_tensor(YA[0:m, c, halves[h]], YA[0:m, c, halves[h]], RES[0:m, 1, halves[h]],
                                            ALU.mult).then_inc(m_n, 1)
            for h in range(2):
                for c, m in enumerate(CT):
                    dve.wait_ge(m_ge, 2 * h + c + 1)
                    nc.vector.tensor_tensor(X[0:m, c, halves[h]], X[0:m, c, halves[h]], YA[0:m, c, halves[h]],
                                            ALU.add).then_inc(m_x, 1)
                if h == 0:
                    dve.wait_ge(m_x, 2)
                    norm_stats(0)

        def scan_pool(pool):
            pool.wait_ge(m_t, 3)
            for i, t in enumerate(READY[:3]):
                pool.wait_ge(m_dt, i + 1)
                pool.tensor_tensor(DU[:, t, :], DT[:, t, :], source(t), ALU.mult).then_inc(m_du, 1)
            for g in range(3):
                if g > 0:
                    pool.wait_ge(m_hc[g - 1], 2 * N + 2)
                pool.sem_inc(m_hc[g], 2)
                with pool.Fori(0, N) as n:
                    for e in range(2):
                        pool.wait_ge(m_h[g], 2 * n + (e + 3))
                        pool.wait_ge(m_cc[g], 2 * n + (e + 2))
                        pool.wait_ge(m_y[g], 2 * n + (e + 1))
                        pool.tensor_tensor(hc[:, e, :], hs[:, e, :], Cs[:, e, :], ALU.mult).then_inc(m_hc[g], 1)
            pool.wait_ge(m_yc, 2)
            pool.tensor_tensor(YA[:, 0, :].rearrange("p (h w) -> p h w", w=W), YA[:, 0, :].rearrange(
                "p (h w) -> p h w", w=W), YS[:, :].rearrange("p (w h) -> p h w", h=H), ALU.add).then_inc(m_ys, 1)

        used[0] = 0
        XP = area([2, PAD * PAD])
        CD = area([9, 128])
        S = [area([2, L]) for _ in range(2)]
        M8 = area([2, 5, 8])
        XPv = XP.rearrange("p t (h w) -> p t h w", w=PAD)

        k_z = sem("conv_border_cleared")
        k_cd = sem("conv_taps_ready")
        k_s = sem("conv_psum_ready")
        k_sc = sem("conv_scores_ready")
        k_m = sem("topk_steps")
        k_x = sem("conv_added")

        def conv_pe(pe):
            pe.wait_ge(g_xn, 12)
            pe.wait_ge(k_z, 1)
            pe.wait_ge(k_cd, 9)
            for h in range(2):
                for tap in range(9):
                    dy, dx = tap // 3, tap % 3
                    mm = nc.tensor.matmul(ps[1][:, HALF * h:HALF * h + HALF], CD[:, tap, :],
                                          XPv[:, 0, dy + 16 * h:dy + 16 * h + 16, dx:dx + W],
                                          start=(tap == 0), stop=(tap == 8))
            mm.then_inc(k_s, 1)

        def conv_act(act):
            act.wait_ge(k_s, 1)
            nc.scalar.activation(S[0][:, 0, :], ps[1][:], ACT.Identity, bias=v_cb[:, 0:1]).then_inc(k_sc, 1)

        def conv_pool(pool):
            pool.wait_ge(m_y[2], 2 * N + 2)
            pool.memset(XP[:, :, :], 0.0).then_inc(k_z, 1)
            for tap in range(9):
                pool.tensor_scalar(CD[:, tap, :], c_ident[:], v_cw[:, 0, tap:tap + 1], 1.0,
                                   ALU.mult, ALU.mult).then_inc(k_cd, 1)

        def conv_dve(dve):
            k = 0

            def step(ins):
                nonlocal k
                ins.then_inc(k_m, 1)
                k += 1
                dve.wait_ge(k_m, k)

            dve.wait_ge(g_xn, 12)
            acc = S[0][0:64, 1, :].rearrange("p (h w) -> p h w", w=W)
            step(nc.vector.tensor_scalar(acc, XPv[0:64, 1, 0:H, 0:W], v_cw[0:64, 1, 0:1], v_cb[0:64, 1:2],
                                         ALU.mult, ALU.add))
            for tap in range(1, 9):
                step(nc.vector.scalar_tensor_tensor(acc, XPv[0:64, 1, tap // 3:tap // 3 + H, tap % 3:tap % 3 + W],
                                                    v_cw[0:64, 1, tap:tap + 1], acc, ALU.mult, ALU.add))
            for t, n in ((1, CT[1]), (0, CT[0])):
                if t == 0:
                    dve.wait_ge(k_sc, 1)
                rounds = -(-TOP // 8)
                for r in range(rounds):
                    step(nc.vector.max(M8[0:n, t, r, :], S[r % 2][0:n, t, :]))
                    left = TOP - 8 * r
                    if left < 8:
                        step(nc.vector.memset(M8[0:n, t, r, left:8], REPLACED))
                    step(nc.vector.match_replace(S[(r + 1) % 2][0:n, t, :], M8[0:n, t, r, :], S[r % 2][0:n, t, :], REPLACED))
                step(nc.vector.scalar_tensor_tensor(
                    S[1][0:n, t, :].rearrange("p (h w) -> p h w", w=W), S[0][0:n, t, :].rearrange("p (h w) -> p h w", w=W),
                    REPLACED, XPv[0:n, t, 1:1 + H, 1:1 + W], ALU.is_equal, ALU.mult))
                nc.vector.tensor_tensor(X[0:n, t, :], X[0:n, t, :], S[1][0:n, t, :], ALU.add).then_inc(k_x, 1)

        used[0] = 0
        Z = area([ZT, L])
        at_cp = used[0]
        CP = area([4, PAD * PAD])
        CPv = CP.rearrange("p t (h w) -> p t h w", w=PAD)
        assert ZT * L + ZT * HALF <= 4 * PAD * PAD
        Y = arena[:, at_cp:at_cp + ZT * L].rearrange("p (t l) -> p t l", t=ZT)
        SQ = arena[:, at_cp + ZT * L:at_cp + ZT * (L + HALF)].rearrange("p (t l) -> p t l", t=ZT)
        XC = area([ZT, L])
        Bn = area([L])
        Cn = area([L])
        dtT = area([NCH, NH])
        e_t = area([NCH * NH])
        dAT = area([NCH * NH])
        dAR = area([NCH, STACK])
        csp = area([L], BF16)
        csl = area([L], BF16)
        csi = area([L], BF16)
        csres = area([L])
        csmid = area([L], BF16)
        cst = area([NCH * NH])
        dte = area([NCH * NH])
        dec = area([NCH * NH])
        XDT = area([2, DI])
        XW = area([2, DI])
        BT = area([2, NS])
        csb = area([2, NH * Q], BF16)
        EX = area([2, NH * Q])
        prev = area([2, DI])
        st_t = area([DI])
        ECS = area([2, DI])
        t1 = area([DI])
        rs = area([HALF])
        POOL_ROWS = 20
        taps2 = area([2, POOL_ROWS * W])

        b_z = sem("mix_border_cleared")
        b_zp = sem("mix_inproj_psum_ready")
        b_zc = sem("mix_inproj_copied")
        b_zh = sem("mix_z_half_psum_ready")
        b_zhc = sem("mix_z_half_copied")
        b_cp = sem("mix_conv_psum_ready")
        b_si = sem("mix_silu_ready")
        b_dp = sem("mix_dt_psum_ready")
        b_d1 = sem("mix_dt_biased")
        b_d2 = sem("mix_dt_clamped")
        b_d3 = sem("mix_dt_softplus")
        b_dt = sem("mix_dt_ready")
        b_da = sem("mix_da_ready")
        b_cs = sem("mix_cumsum_psum_ready")
        b_csc = sem("mix_cumsum_copied")
        b_dif = sem("mix_decay_exponent")
        b_dec = sem("mix_decays_ready")
        b_tr = sem("mix_tokens_psum_ready")
        b_bt = sem("mix_b_tokens_copied")
        b_xdt = sem("mix_xdt_ready")
        b_xw = sem("mix_weighted_x_ready")
        b_csb = sem("mix_cumsum_blocks_ready")
        b_ex = sem("mix_exponents_psum_ready")
        b_exc = sem("mix_exp_ready")
        b_att = sem("mix_att_ready")
        b_y = sem("mix_chunk_psum_ready")
        b_ec = sem("mix_inter_decay_ready")
        b_y1 = sem("mix_inter_scaled")
        b_yc = sem("mix_chunk_ready")
        b_pd = sem("mix_state_decayed")
        b_pr = sem("mix_state_ready")
        b_yx = sem("mix_skip_added")
        b_mu = sem("mix_mean_ready")
        b_ce = sem("mix_centred")
        b_sq = sem("mix_squares_ready")
        b_va = sem("mix_var_ready")
        b_sd = sem("mix_std_ready")
        b_n = sem("mix_scaled")
        b_xm = sem("mix_pool_products")
        b_xs = sem("mix_pool_products_added")
        b_hi = sem("mix_cumsum_high_parts")
        b_res = sem("mix_cumsum_rests")
        b_mid = sem("mix_cumsum_middle_parts")
        b_lo = sem("mix_cumsum_low_parts")
        b_st = sem("mix_cumsum_stacks_ready")
        b_csb0 = sem("mix_first_cumsum_block_ready")
        b_tap = sem("mix_taps_added")
        b_xv = sem("mix_convolved")
        b_gz = sem("mix_gated")
        b_o = sem("mix_outproj_ready")
        b_x = sem("mix_added")

        def tokens(c):
            return slice(Q * c, Q * c + Q)

        def half(h):
            return slice(HALF * h, HALF * h + HALF)

        PROJ = (0, 3, 1, 2, 4)
        PROJ_PS = (0, 1, 3, 0, 1)
        AHEAD = 5

        def mix_pe(pe):
            def project(s):
                i, p = PROJ[s], PROJ_PS[s]
                w, lo, n = (w_x, 128 * i, 128 if i < 3 else 64) if i < 4 else (w_z, 128 * (i - 4), 128)
                before = [q for q in range(s) if PROJ_PS[q] == p]
                if before:
                    pe.wait_ge(b_zc, before[-1] + 1)
                for h in range(2):
                    pe.wait_ge(g_xn, 12 + 2 * (h + 1))
                    for c, m in enumerate(CT):
                        mm = nc.tensor.matmul(ps[p][0:n, half(h)], w[0:m, c, lo:lo + n],
                                              XN[0:m, c, half(h)], start=(c == 0), stop=(c == 1))
                mm.then_inc(b_zp, 1)

            for s in range(5):
                project(s)
                if s == 2:
                    for j in range(NCH):
                        for c, m in enumerate(CT):
                            mm = nc.tensor.matmul(ps[2][:, NH * j:NH * j + NH], XN[0:m, c, tokens(j)],
                                                  w_dt3[0:m, c, :], start=(c == 0), stop=(c == 1))
                    mm.then_inc(b_dp, 1)
            def conv_bc(taps):
                for h, tap in taps:
                    dy, dx = tap // 3, tap % 3
                    mm = nc.tensor.matmul(ps[3][0:64, half(h)], diag[:, tap, :],
                                          CPv[0:64, 3, dy + 16 * h:dy + 16 * h + 16, dx:dx + W],
                                          start=(tap == 0), stop=(tap == 8))
                return mm

            pe.wait_ge(b_zc, 3)
            taps = [(h, tap) for h in range(2) for tap in range(9)]
            conv_bc(taps[:AHEAD])
            pe.wait_ge(b_da, 7)
            pe.wait_ge(b_d1, 1)
            for c in range(NCH):
                mm = nc.tensor.matmul(ps[2][0:STACK, tokens(c)], dAR[:, c, :], c_upper[:], start=True, stop=True)
            mm.then_inc(b_cs, 1)
            pe.wait_ge(b_zc, 5)
            nc.tensor.matmul(ps[1][:, 0:96], c_upper[:], dAT[:, :], start=True, stop=True)
            nc.tensor.matmul(ps[1][:, 128:224], c_ones[:], dAT[:, :], start=True, stop=True).then_inc(b_cs, 1)
            conv_bc(taps[AHEAD:]).then_inc(b_cp, 1)

            def turn(c):
                if c >= 1:
                    pe.wait_ge(b_xdt, c)
                    pe.wait_ge(b_att, c)
                for t in range(ZT):
                    nc.tensor.transpose(ps[3][:, 128 * t:128 * t + 128], XC[:, t, tokens(c)], c_ident[:])
                nc.tensor.matmul(ps[3][:, DI:DI + Q], Bn[0:32, tokens(c)], Cn[0:32, tokens(c)],
                                 start=True, stop=True).then_inc(b_tr, 1)

            def exponents(c):
                if c >= 1:
                    pe.wait_ge(b_csb, c)
                    pe.wait_ge(b_exc, c)
                else:
                    pe.wait_ge(b_csb0, 1)
                for g in range(3):
                    P = (ps[0][:, 0:HALF], ps[0][:, HALF:L], ps[1][:, 0:HALF])[g]
                    nc.tensor.matmul(P, csl[0:STACK, tokens(c)], csb[0:STACK, c % 2, HALF * g:HALF * g + HALF],
                                     start=True, stop=False)
                    mm = nc.tensor.matmul(P, c_identb[:], c_mask[:].unsqueeze(1).to_broadcast([128, 4, Q]),
                                          start=False, stop=True)
                mm.then_inc(b_ex, 1)

            def norm_sum(h, src, ready, count, done):
                pe.wait_ge(ready, count)
                if h == 1:
                    pe.wait_ge(b_sd, 1)
                for t in range(ZT):
                    mm = nc.tensor.matmul(ps[1][:, HALF:L], c_mean[:], src[:, t, :],
                                          start=(t == 0), stop=(t == ZT - 1))
                mm.then_inc(done, 1)

            def out_proj(h):
                if h == 0:
                    pe.wait_ge(b_exc, NCH)
                for t in range(ZT):
                    pe.wait_ge(b_gz, ZT * h + t + 1)
                    for o, n in enumerate(CT):
                        if h == 1 and t == 0:
                            pe.wait_ge(b_x, o + 1)
                        mm = nc.tensor.matmul(ps[0][0:n, half(o)], w_o[:, t, 128 * o:128 * o + n], Y[:, t, half(h)],
                                              start=(t == 0), stop=(t == ZT - 1))
                        if t == ZT - 1:
                            mm.then_inc(b_o, 1)

            pe.wait_ge(b_csc, 2)
            exponents(0)
            pe.wait_ge(b_si, 5)
            turn(0)
            for c in range(NCH):
                if c >= 1:
                    pe.wait_ge(b_pr, c)
                    pe.wait_ge(b_bt, c)
                for t in range(ZT):
                    nc.tensor.matmul(ps[2][:, 128 * t:128 * t + 128], prev[0:32, c % 2, 128 * t:128 * t + 128],
                                     Cn[0:32, tokens(c)], start=True, stop=True)
                nc.tensor.transpose(ps[2][:, DI:DI + NS], Bn[0:32, tokens(c)], c_ident[0:32, 0:32])
                for t in range(ZT):
                    mm = nc.tensor.matmul(ps[3][:, HALF + 128 * t:HALF + 128 * t + 128],
                                          c_selhead[:, 128 * t:128 * t + 128], csp[0:STACK, tokens(c)],
                                          start=True, stop=True)
                mm.then_inc(b_y, 1)
                if c + 1 < NCH:
                    turn(c + 1)
                    exponents(c + 1)
                pe.wait_ge(b_att, c + 1)
                pe.wait_ge(b_xdt, c + 1)
                if c >= 1:
                    pe.wait_ge(b_yc, c)
                for h in range(NH):
                    r = HP * (h % 4)
                    mm = nc.tensor.matmul(ps[2][r:r + HP, HALF + 128 * (h // 4):HALF + 128 * (h // 4) + 128],
                                          XDT[:, c % 2, HP * h:HP * h + HP], EX[:, c % 2, Q * h:Q * h + Q],
                                          start=True, stop=True)
                mm.then_inc(b_y, 1)
                pe.wait_ge(b_xw, c + 1)
                pe.wait_ge(b_bt, c + 1)
                pe.wait_ge(b_ec, c + 1)
                nc.tensor.matmul(ps[3][0:32, HALF:HALF + DI], BT[:, c % 2, :], XW[:, c % 2, :],
                                 start=True, stop=True).then_inc(b_y, 1)
                if c < NCH // 2:
                    if c >= 1:
                        pe.wait_ge(b_zhc, c)
                    for k, m in enumerate(CT):
                        mm = nc.tensor.matmul(ps[1][:, HALF:L], w_z[0:m, k, 128 * (1 + c // 2):128 * (2 + c // 2)],
                                              XN[0:m, k, half(c % 2)], start=(k == 0), stop=(k == 1))
                    mm.then_inc(b_zh, 1)
                if c == NCH // 2:
                    pe.wait_ge(b_zhc, NCH // 2)
                    norm_sum(0, Y[:, :, half(0)], b_yx, NCH // 2, b_mu)
                if c == NCH // 2 + 1:
                    norm_sum(0, SQ, b_sq, 1, b_va)
            norm_sum(1, Y[:, :, half(1)], b_yx, NCH, b_mu)
            out_proj(0)
            norm_sum(1, SQ, b_sq, 2, b_va)
            out_proj(1)

        def mix_act(act):
            act.wait_ge(b_z, 2)

            def projected(s):
                act.wait_ge(b_zp, s + 1)
                i, p = PROJ[s], PROJ_PS[s]
                n = 64 if i == 3 else 128
                if i < 4:
                    nc.scalar.activation(CPv[0:n, i, 1:1 + H, 1:1 + W], ps[p][0:n, :].rearrange(
                        "p (h w) -> p h w", w=W), ACT.Copy).then_inc(b_zc, 1)
                else:
                    nc.scalar.activation(Z[:, i - 4, :], ps[p][:], ACT.Copy).then_inc(b_zc, 1)

            for s in range(4):
                projected(s)
            act.wait_ge(b_d2, 1)
            nc.scalar.activation(e_t[:, :], e_t[:, :], ACT.Exp).then_inc(b_d3, 1)
            act.wait_ge(b_d3, 1)
            nc.scalar.activation(e_t[:, :], e_t[:, :], ACT.Ln, bias=1.0).then_inc(b_d3, 1)
            projected(4)
            act.wait_ge(b_cs, 1)
            nc.scalar.activation(csp[0:STACK, :], ps[2][0:STACK, :], ACT.Copy).then_inc(b_hi, 1)
            act.wait_ge(b_res, 1)
            nc.scalar.activation(csp[32:64, :], csres[32:64, :], ACT.Copy).then_inc(b_mid, 1)
            nc.scalar.activation(csmid[64:STACK, :], csres[64:STACK, :], ACT.Copy).then_inc(b_mid, 1)
            for t in range(ZT):
                if t == 2:
                    act.wait_ge(b_cp, 1)
                    nc.scalar.activation(Bn[0:32, :], ps[3][0:32, :], ACT.Silu, bias=v_mcb[0:32, 3:4]).then_inc(b_si, 1)
                    nc.scalar.activation(Cn[0:32, :], ps[3][32:64, :], ACT.Silu, bias=v_mcbC[:]).then_inc(b_si, 1)
                act.wait_ge(b_xv, t + 1)
                if t == 2:
                    act.wait_ge(b_xs, 8)
                nc.scalar.activation(XC[:, t, :], XC[:, t, :], ACT.Silu, bias=v_mcb[:, t:t + 1]).then_inc(b_si, 1)
            act.wait_ge(b_dif, 1)
            nc.scalar.activation(dte[:, :], dte[:, :], ACT.Exp).then_inc(b_dec, 1)
            nc.scalar.activation(dec[:, :], dec[:, :], ACT.Exp).then_inc(b_dec, 1)

            def decays(c):
                act.wait_ge(b_ex, c + 1)
                if c >= 2:
                    act.wait_ge(b_y, 3 * (c - 1) - 1)
                nc.scalar.activation(EX[:, c % 2, 0:L], ps[0][:], ACT.Exp)
                nc.scalar.activation(EX[:, c % 2, L:L + HALF], ps[1][:, 0:HALF], ACT.Exp).then_inc(b_exc, 1)

            def squares(h):
                act.wait_ge(b_ce, h + 1)
                if h == 1:
                    act.wait_ge(b_va, 1)
                nc.scalar.activation(SQ[:, :, :], Y[:, :, half(h)], ACT.Square).then_inc(b_sq, 1)

            def scale(h):
                act.wait_ge(b_va, h + 1)
                if h == 1:
                    act.wait_ge(b_n, ZT)
                nc.scalar.activation(rs[:, :], ps[1][:, HALF:L], ACT.Ln, bias=v_eps5[:], scale=C / DI).then_inc(b_sd, 1)
                act.wait_ge(b_sd, 2 * h + 1)
                nc.scalar.activation(rs[:, :], rs[:, :], ACT.Exp, scale=-0.5).then_inc(b_sd, 1)

            decays(0)
            for c in range(NCH):
                act.wait_ge(b_y, 3 * c + 1)
                if c >= 2:
                    act.wait_ge(b_y1, c - 1)
                nc.scalar.activation(ECS[:, c % 2, :], ps[3][:, HALF:HALF + DI], ACT.Exp).then_inc(b_ec, 1)
                if c + 1 < NCH:
                    decays(c + 1)
                if 1 <= c <= NCH // 2:
                    act.wait_ge(b_zh, c)
                    nc.scalar.activation(Z[:, 1 + (c - 1) // 2, half((c - 1) % 2)], ps[1][:, HALF:L],
                                         ACT.Copy).then_inc(b_zhc, 1)
                if c == NCH // 2 + 1:
                    squares(0)
                if c == NCH // 2 + 2:
                    scale(0)
            squares(1)
            scale(1)

        def blocks(eng, c, done):
            eng.tensor_tensor(csb[0:STACK, c % 2, :].rearrange("p (h q) -> p h q", q=Q),
                              csi[0:STACK, tokens(c)].unsqueeze(1).to_broadcast([STACK, NH, Q]),
                              c_heads[:, 0:NH].unsqueeze(2).to_broadcast([STACK, NH, Q]), ALU.mult).then_inc(done, 1)

        def image_rows(t, lo, hi, tap):
            return CPv[:, t, lo + tap // 3:hi + tap // 3, tap % 3:tap % 3 + W]

        def convolve(t, taps, lo=0):
            dve = nc.vector
            acc = XC[:, t, :].rearrange("p (h w) -> p h w", w=W)[:, lo:H, :]
            for tap in taps:
                src, w = image_rows(t, lo, H, tap), v_mcw[:, t, tap:tap + 1]
                if tap == 0:
                    dve.tensor_scalar(acc, src, w, None, ALU.mult).then_inc(b_tap, 1)
                else:
                    dve.wait_ge(b_tap, 8 * t + tap)
                    dve.scalar_tensor_tensor(acc, src, w, acc, ALU.mult, ALU.add).then_inc(
                        b_xv if tap == 8 else b_tap, 1)

        def convolve_pool(pool):
            acc = XC[:, 2, :].rearrange("p (h w) -> p h w", w=W)[:, 0:POOL_ROWS, :]
            for tap in range(9):
                dst = acc if tap == 0 else taps2[:, tap % 2, :].rearrange("p (h w) -> p h w", w=W)
                if tap >= 3:
                    pool.wait_ge(b_xs, tap - 2)
                pool.tensor_scalar(dst, image_rows(2, 0, POOL_ROWS, tap), v_mcw[:, 2, tap:tap + 1], 1.0,
                                   ALU.mult, ALU.mult).then_inc(b_xm, 1)
                if tap >= 1:
                    pool.wait_ge(b_xm, tap + 1)
                    if tap >= 2:
                        pool.wait_ge(b_xs, tap - 1)
                    pool.tensor_tensor(acc, acc, dst, ALU.add).then_inc(b_xs, 1)

        def mix_dve(dve):
            def heads(v):
                return v.unsqueeze(2).to_broadcast([v.shape[0], NH, HP])

            dve.wait_ge(b_zc, 1)
            convolve(0, range(9))
            dve.wait_ge(b_dp, 1)
            bias = v_dtb3[:].unsqueeze(1).to_broadcast([128, NCH, NH])
            e3 = e_t.rearrange("p (c h) -> p c h", h=NH)
            nc.vector.tensor_tensor(dtT[:, :, :], ps[2][:, 0:96].rearrange("p (c h) -> p c h", h=NH), bias,
                                    ALU.add).then_inc(b_d1, 1)
            dve.wait_ge(b_d1, 1)
            nc.vector.tensor_scalar(e3, dtT[:, :, :], SOFTPLUS_LINEAR, None, ALU.min).then_inc(b_d2, 1)
            dve.wait_ge(b_zc, 3)
            convolve(1, range(0, 4))
            dve.wait_ge(b_d3, 2)
            nc.vector.tensor_tensor(dtT[:, :, :], dtT[:, :, :], e3, ALU.max).then_inc(b_dt, 1)
            dve.wait_ge(b_dt, 1)
            na = v_na3[:].unsqueeze(1).to_broadcast([128, NCH, NH])
            da3 = dAT.rearrange("p (c h) -> p c h", h=NH)
            nc.vector.tensor_tensor(da3, dtT[:, :, :], na, ALU.mult).then_inc(b_da, 1)
            dve.wait_ge(b_da, 1)
            dve.wait_ge(b_z, 3)
            for sign in range(2):
                for p in range(3):
                    at = 32 * p + NH * sign
                    nc.vector.tensor_scalar(dAR[:, :, at:at + NH], da3, 1.0 - 2.0 * sign, None,
                                            ALU.mult).then_inc(b_da, 1)
            convolve(1, range(4, 9))
            dve.wait_ge(b_hi, 1)
            nc.vector.tensor_tensor(csres[0:STACK, :], ps[2][0:STACK, :], csp[0:STACK, :], ALU.subtract).then_inc(b_res, 1)
            dve.wait_ge(b_cs, 2)
            nc.vector.tensor_copy(cst[:, :], ps[1][:, 0:96]).then_inc(b_csc, 1)
            nc.vector.tensor_copy(dec[:, :], ps[1][:, 128:224]).then_inc(b_csc, 1)
            dve.wait_ge(b_csc, 2)
            nc.vector.tensor_tensor(dte[:, :], dec[:, :], cst[:, :], ALU.subtract).then_inc(b_dif, 1)
            dve.wait_ge(b_mid, 2)
            dve.wait_ge(b_res, 1)
            nc.vector.tensor_tensor(csp[64:STACK, :], csres[64:STACK, :], csmid[64:STACK, :], ALU.subtract).then_inc(b_lo, 1)
            dve.wait_ge(b_lo, 1)
            for dst, own, ones_ in ((csi, NH, NH + 1), (csl, NH + 1, NH)):
                nc.vector.tensor_scalar(dst[0:STACK, :], csp[0:STACK, :], c_heads[:, own:own + 1],
                                        c_heads[:, ones_:ones_ + 1], ALU.mult, ALU.add).then_inc(b_st, 1)
            dve.wait_ge(b_st, 1)
            blocks(nc.vector, 0, b_csb0)
            dve.wait_ge(b_zc, 4)
            convolve(2, range(9), POOL_ROWS)

            def scaled_x(c):
                dve.wait_ge(b_tr, c + 1)
                if c >= 2:
                    dve.wait_ge(b_y, 3 * (c - 1) - 1)
                    dve.wait_ge(b_xw, c - 1)
                nc.vector.tensor_tensor(XDT[:, c % 2, :].rearrange("p (h q) -> p h q", q=HP),
                                        ps[3][:, 0:DI].rearrange("p (h q) -> p h q", q=HP), heads(dtT[:, c, :]),
                                        ALU.mult).then_inc(b_xdt, 1)

            def attention(c):
                dve.wait_ge(b_exc, c + 1)
                dve.wait_ge(b_tr, c + 1)
                att = EX[:, c % 2, :].rearrange("p (h q) -> p h q", q=Q)
                nc.vector.tensor_tensor(att, att, ps[3][:, DI:DI + Q].unsqueeze(1).to_broadcast([128, NH, Q]),
                                        ALU.mult).then_inc(b_att, 1)

            def centre(h):
                y = Y[:, :, half(h)]
                dve.wait_ge(b_mu, h + 1)
                nc.vector.scalar_tensor_tensor(y, ps[1][:, HALF:L].unsqueeze(1).to_broadcast([128, ZT, HALF]),
                                               -C / DI, y, ALU.mult, ALU.add).then_inc(b_ce, 1)

            def finish(h):
                dve.wait_ge(b_sd, 2 * h + 2)
                dve.wait_ge(b_sq, h + 1)
                for t in range(ZT + 1):
                    if t < ZT:
                        y = Y[:, t, half(h)]
                        nc.vector.scalar_tensor_tensor(y, y, v_nw[:, t:t + 1], rs[:, :], ALU.mult,
                                                       ALU.mult).then_inc(b_n, 1)
                    if t >= 1:
                        y = Y[:, t - 1, half(h)]
                        dve.wait_ge(b_n, ZT * h + t)
                        nc.vector.scalar_tensor_tensor(y, y, v_nb[:, t - 1:t], Z[:, t - 1, half(h)], ALU.add,
                                                       ALU.mult).then_inc(b_gz, 1)

            def added(h):
                for o, n in enumerate(CT):
                    dve.wait_ge(b_o, 2 * h + o + 1)
                    xs = X[0:n, o, half(h)]
                    nc.vector.tensor_tensor(xs, xs, ps[0][0:n, half(o)], ALU.add).then_inc(b_x, 1)

            scaled_x(0)
            attention(0)
            for c in range(NCH):
                if c >= 1:
                    dve.wait_ge(b_pr, c)
                nc.vector.tensor_tensor(st_t[0:32, :].rearrange("p (h q) -> p h q", q=HP),
                                        prev[0:32, c % 2, :].rearrange("p (h q) -> p h q", q=HP),
                                        heads(dec[0:32, NH * c:NH * c + NH]), ALU.mult).then_inc(b_pd, 1)
                dve.wait_ge(b_ec, c + 1)
                nc.vector.tensor_tensor(t1[:, :], ps[2][:, 0:DI], ECS[:, c % 2, :], ALU.mult).then_inc(b_y1, 1)
                if c >= 2:
                    dve.wait_ge(b_y, 3 * (c - 1))
                nc.vector.tensor_copy(BT[:, c % 2, :], ps[2][:, DI:DI + NS]).then_inc(b_bt, 1)
                if c + 1 < NCH:
                    scaled_x(c + 1)
                dve.wait_ge(b_y1, c + 1)
                dve.wait_ge(b_y, 3 * c + 2)
                nc.vector.tensor_tensor(Y[:, :, tokens(c)], ps[2][:, HALF:HALF + DI].rearrange("p (t q) -> p t q", q=Q),
                                        t1.rearrange("p (t q) -> p t q", q=Q), ALU.add).then_inc(b_yc, 1)
                dve.wait_ge(b_y, 3 * c + 3)
                dve.wait_ge(b_pd, c + 1)
                nc.vector.tensor_tensor(prev[0:32, (c + 1) % 2, :], ps[3][0:32, HALF:HALF + DI], st_t[0:32, :],
                                        ALU.add).then_inc(b_pr, 1)
                dve.wait_ge(b_yc, c + 1)
                for t in range(ZT):
                    y = Y[:, t, tokens(c)]
                    ins = nc.vector.scalar_tensor_tensor(y, XC[:, t, tokens(c)], v_d3[:, t:t + 1], y, ALU.mult, ALU.add)
                ins.then_inc(b_yx, 1)
                if c + 1 < NCH:
                    attention(c + 1)
                if c == NCH // 2:
                    centre(0)
                if c == NCH // 2 + 2:
                    finish(0)
            centre(1)
            added(0)
            finish(1)
            added(1)

        def mix_pool(pool):
            pool.wait_ge(k_x, 2)
            pool.memset(CP[:, :, :], 0.0).then_inc(b_z, 1)
            pool.memset(prev[0:32, 0, :], 0.0).then_inc(b_z, 1)
            pool.memset(dAR[:, :, :], 0.0).then_inc(b_z, 1)
            pool.wait_ge(b_zc, 4)
            convolve_pool(pool)
            pool.wait_ge(b_st, 2)
            pool.wait_ge(b_dec, 1)
            for c in range(NCH):
                if c + 1 < NCH:
                    if c >= 1:
                        pool.wait_ge(b_ex, c)
                    blocks(pool, c + 1, b_csb)
                pool.wait_ge(b_xdt, c + 1)
                if c >= 2:
                    pool.wait_ge(b_y, 3 * (c - 1))
                pool.tensor_tensor(XW[:, c % 2, :].rearrange("p (h q) -> p h q", q=HP),
                                   XDT[:, c % 2, :].rearrange("p (h q) -> p h q", q=HP),
                                   dte[:, NH * c:NH * c + NH].unsqueeze(2).to_broadcast([128, NH, HP]),
                                   ALU.mult).then_inc(b_xw, 1)

        done, dones = [(a_x, 4), (m_x, 4), (k_x, 2), (b_x, 4)][phases - 1]

        with nc.Block() as block:
            @block.sync
            def _(sp):
                for c, m in enumerate(CT):
                    sp.dma_start(XI[0:m, c, :], x[0, 128 * c:128 * c + m, :]).then_inc(s_x, 16)
                sp.sem_inc(s_out, 1)

        with nc.Fori(0, n_batch) as b:
            with nc.Block() as block:
                @block.sync
                def _(sp):
                    attn_sp(sp)
                    sp.wait_ge(a_x, 4)
                    for c, m in enumerate(CT):
                        sp.dma_start(XI[0:m, c, :], x[b + 1, 128 * c:128 * c + m, :]).then_inc(s_x, 16)
                    if phases > 1:
                        scan_sp(sp)
                    sp.wait_ge(done, dones)
                    for c, m in enumerate(CT):
                        sp.dma_start(out[b, 128 * c:128 * c + m, :], X[0:m, c, :]).then_inc(s_out, 16)

                @block.tensor
                def _(pe):
                    norm_pe(pe, 0)
                    pe.wait_ge(a_one, 2)
                    attn_pe(pe)
                    if phases > 1:
                        norm_pe(pe, 1)
                        scan_pe(pe)
                    if phases > 2:
                        norm_pe(pe, 2)
                        conv_pe(pe)
                    if phases > 3:
                        norm_pe(pe, 3)
                        mix_pe(pe)

                @block.scalar
                def _(act):
                    norm_act(act, 0)
                    attn_act(act)
                    if phases > 1:
                        norm_act(act, 1)
                        scan_act(act)
                    if phases > 2:
                        norm_act(act, 2)
                        conv_act(act)
                    if phases > 3:
                        norm_act(act, 3)
                        mix_act(act)

                @block.vector
                def _(dve):
                    dve.wait_ge(s_x, 32 * b + 32)
                    norm_dve(dve, 0, lambda t, n: XN[0:n, t, :], x_in=XI)
                    attn_dve(dve, b)
                    if phases > 1:
                        dve.wait_ge(a_x, 4)
                        norm_dve(dve, 1, lambda t, n: XN[0:n, t, :], begun=True)
                        scan_dve(dve)
                    if phases > 2:
                        dve.wait_ge(m_x, 4)
                        norm_dve(dve, 2, lambda t, n: XPv[0:n, t, 1:1 + H, 1:1 + W], begun=True, room=k_z)
                        conv_dve(dve)
                    if phases > 3:
                        dve.wait_ge(k_x, 2)
                        norm_dve(dve, 3, lambda t, n: XN[0:n, t, :])
                        mix_dve(dve)

                @block.gpsimd
                def _(pool):
                    attn_pool(pool)
                    if phases > 1:
                        scan_pool(pool)
                    if phases > 2:
                        conv_pool(pool)
                    if phases > 3:
                        mix_pool(pool)

            engines = (nc.sync, nc.tensor, nc.vector, nc.scalar, nc.gpsimd)
            for i, s in enumerate(sems):
                engines[i % len(engines)].sem_clear(s)
            nc.all_engine_barrier()

        with nc.Block() as block:
            @block.sync
            def _(sp):
                sp.wait_ge(s_x, 32 * (n_batch + 1))
                sp.wait_ge(s_out, 32 * n_batch + 1)


def layout(inp):
    import numpy as np

    f = {k: np.ascontiguousarray(v) for k, v in inp.items()}
    wqkv = f["L0_conv_qkv_w"].T

    def stacks(xp):
        o = np.zeros((C, K, 102), xp.dtype)
        for s in range(K):
            g, j = s // 2, s % 2
            for part in range(3):
                for i in range(2):
                    at = 32 * part + 16 * i
                    o[:, s, at:at + N] = xp[:, g + 2 * i, R + N * j:R + N * j + N]
            o[:, s, 96:96 + R] = xp[:, g + 2 * j, :R]
        return o

    xp = f["L1_conv_x_proj_weight"].transpose(2, 0, 1)
    ipw = f["L3_conv_in_proj_w"].T
    d = {
        "x": np.concatenate([f["x"], f["x"][:1]]).reshape(B + 1, C, L),
        "wqk": np.concatenate([wqkv[:, :128], wqkv[:, C:C + 128], wqkv[:, 128:C], wqkv[:, C + 128:2 * C]], 1), "wv": wqkv[:, 2 * C:],
        "wp": f["L0_conv_proj_w"].T, "pb": f["L0_conv_proj_b"],
        "xpw": stacks(xp),
        "dtw": f["L1_conv_dt_projs_weight"].transpose(2, 0, 1),
        "dtb": f["L1_conv_dt_projs_bias"], "alog": f["L1_conv_A_logs"].reshape(K, C, N),
        "ds": f["L1_conv_Ds"].reshape(K, C), "lnw": f["L1_conv_ln_weight"], "lnb": f["L1_conv_ln_bias"],
        "cw": f["L2_conv_weight"].reshape(C, 9), "cb": f["L2_conv_bias"],
        "wz": ipw[:, :DI], "wx": ipw[:, DI:2 * DI + 2 * NS], "wdt": ipw[:, 2 * DI + 2 * NS:],
        "mcw": f["L3_conv_conv_w"].reshape(DI + 2 * NS, 9), "mcb": f["L3_conv_conv_b"],
        "dtb3": f["L3_conv_dt_bias"], "alog3": f["L3_conv_A_log"], "d3": f["L3_conv_D"],
        "nw": f["L3_conv_norm_w"], "nb": f["L3_conv_norm_b"], "wo": f["L3_conv_out_proj_w"].T,
    }
    return {k: np.ascontiguousarray(v) for k, v in d.items()}


def kernel(**inputs):
    import numpy as np
    import concourse.bacc as bacc
    from concourse.bass_utils import run_bass_kernel_spmd

    nc = bacc.Bacc("TRN2", target_bir_lowering=False, num_devices=1)
    arrays, args = {}, {}
    for name, a in {**layout(inputs), **consts()}.items():
        arrays[f"in_{name}"] = a
        args[name] = nc.dram_tensor(f"in_{name}", a.shape, mybir.dt.from_np(a.dtype), kind="ExternalInput").ap()
    args["out"] = nc.dram_tensor("out_x", (B, C, L), F32, kind="ExternalOutput").ap()
    build(nc, **args)
    r = run_bass_kernel_spmd(nc, [arrays], core_ids=[0])
    return r.results[0]["out_x"].reshape(B, C, H, W)
```
